# Optimizing a Trainium2 kernel written in Bass

```python
import numpy as np
import jax
import jax.numpy as jnp

def _softmax(x, axis=-1):
    return jax.nn.softmax(x, axis=axis)

def _gelu(x):
    return jax.nn.gelu(x, approximate=True)

def _silu(x):
    return jax.nn.silu(x)

def _sigmoid(x):
    return jax.nn.sigmoid(x)

def _layernorm(x, axis=-1, eps=1e-05):
    m = jnp.mean(x, axis=axis, keepdims=True)
    v = jnp.var(x, axis=axis, keepdims=True)
    return (x - m) / jnp.sqrt(v + eps)

def _scatter_add(tgt, idx, src, axis=0):
    return tgt.at[idx].add(src)

def _segment_sum(src, seg, n):
    return jax.ops.segment_sum(src, seg, n)
kernel_name = 'mk_conv_preact_d2_conv_nchw256_r2_dc9fe8'

def setup_inputs(seed: int=0):
    np.random.seed(seed)
    _w = jnp.asarray

    def _rec_inputs():
        import jax
        import jax.numpy as jnp
        _gk = jax.random.key(seed)
        x = -0.000125 + 0.9999 * jax.random.normal(jax.random.fold_in(_gk, 1), (2, 128, 128, 128), jnp.float32)
        return x
    x = _rec_inputs()

    def _L0_conv_setup():
        import jax, jax.numpy as jnp
        import numpy as np
        B, N, D = (2, 128, 128)
        key = jax.random.key(seed)
        ks = jax.random.split(key, 9)
        s = 1.0 / np.sqrt(D)
        return {'pair_repr': jax.random.normal(ks[0], (B, N, N, D), dtype=jnp.float32), 'Wa': jax.random.uniform(ks[1], (D, D), jnp.float32, -s, s), 'ba': jax.random.uniform(ks[2], (D,), jnp.float32, -s, s), 'Wb': jax.random.uniform(ks[3], (D, D), jnp.float32, -s, s), 'bb': jax.random.uniform(ks[4], (D,), jnp.float32, -s, s), 'Wg': jax.random.uniform(ks[5], (D, D), jnp.float32, -s, s), 'bg': jax.random.uniform(ks[6], (D,), jnp.float32, -s, s), 'Wo': jax.random.uniform(ks[7], (D, D), jnp.float32, -s, s), 'bo': jax.random.uniform(ks[8], (D,), jnp.float32, -s, s)}
    _L0_conv_all = _L0_conv_setup()
    _L0_conv_in = {k: v for k, v in _L0_conv_all.items() if k in ('Wa', 'ba', 'Wb', 'bb', 'Wg', 'bg', 'Wo', 'bo')}
    del _L0_conv_all

    def _L1_conv_setup():
        import jax, jax.numpy as jnp
        import numpy as np
        B, C, O, H, W = (8, 128, 128, 32, 32)
        K = 3

        def _bilinear_gather(x, py, px):
            Bb, Cc, Hh, Ww = x.shape
            y0f = jnp.floor(py)
            x0f = jnp.floor(px)
            wy = (py - y0f).reshape(Bb, 1, -1)
            wx = (px - x0f).reshape(Bb, 1, -1)
            y0 = y0f.astype(jnp.int32)
            x0 = x0f.astype(jnp.int32)
            flat = x.reshape(Bb, Cc, Hh * Ww)

            def gather(yi, xi):
                valid = (yi >= 0) & (yi < Hh) & (xi >= 0) & (xi < Ww)
                yc = jnp.clip(yi, 0, Hh - 1)
                xc = jnp.clip(xi, 0, Ww - 1)
                idx = (yc * Ww + xc).reshape(Bb, 1, -1)
                g = jnp.take_along_axis(flat, jnp.broadcast_to(idx, (Bb, Cc, idx.shape[-1])), axis=2)
                return g * valid.reshape(Bb, 1, -1).astype(x.dtype)
            v00 = gather(y0, x0)
            v01 = gather(y0, x0 + 1)
            v10 = gather(y0 + 1, x0)
            v11 = gather(y0 + 1, x0 + 1)
            return v00 * (1 - wy) * (1 - wx) + v01 * (1 - wy) * wx + v10 * wy * (1 - wx) + v11 * wy * wx
        key = jax.random.key(seed)
        k1, k2, k3 = jax.random.split(key, 3)
        x = jax.random.normal(k1, (B, C, H, W), dtype=jnp.float32)
        w_off = jax.random.normal(k2, (2 * K * K, C, K, K), dtype=jnp.float32) * 0.01
        b_off = jnp.zeros((2 * K * K,), dtype=jnp.float32)
        bound = float(np.sqrt(6.0 / (C * K * K + O * K * K)))
        w_def = jax.random.uniform(k3, (O, C, K, K), dtype=jnp.float32, minval=-bound, maxval=bound)
        return {'x': x, 'w_off': w_off, 'b_off': b_off, 'w_def': w_def}
    _L1_conv_all = _L1_conv_setup()
    _L1_conv_in = {k: v for k, v in _L1_conv_all.items() if k in ('w_off', 'b_off', 'w_def')}
    del _L1_conv_all
    return {'x': x, 'L0_conv_Wa': _L0_conv_in['Wa'], 'L0_conv_ba': _L0_conv_in['ba'], 'L0_conv_Wb': _L0_conv_in['Wb'], 'L0_conv_bb': _L0_conv_in['bb'], 'L0_conv_Wg': _L0_conv_in['Wg'], 'L0_conv_bg': _L0_conv_in['bg'], 'L0_conv_Wo': _L0_conv_in['Wo'], 'L0_conv_bo': _L0_conv_in['bo'], 'L1_conv_w_off': _L1_conv_in['w_off'], 'L1_conv_b_off': _L1_conv_in['b_off'], 'L1_conv_w_def': _L1_conv_in['w_def']}

def reference(x, L0_conv_Wa, L0_conv_ba, L0_conv_Wb, L0_conv_bb, L0_conv_Wg, L0_conv_bg, L0_conv_Wo, L0_conv_bo, L1_conv_w_off, L1_conv_b_off, L1_conv_w_def):
    import jax
    import jax.numpy as jnp

    def _L0_conv_ref(pair_repr, Wa, ba, Wb, bb, Wg, bg, Wo, bo):
        import jax, jax.numpy as jnp
        import numpy as np
        B, N, D = (2, 128, 128)
        a = pair_repr @ Wa + ba
        b = pair_repr @ Wb + bb
        g = jax.nn.sigmoid(pair_repr @ Wg + bg)
        ab = jnp.einsum('bijk,bikl->bijl', a, b)
        return g * ab @ Wo + bo

    def _L1_conv_ref(x, w_off, b_off, w_def):
        import jax, jax.numpy as jnp
        import numpy as np
        B, C, O, H, W = (8, 128, 128, 32, 32)
        K = 3

        def _bilinear_gather(x, py, px):
            Bb, Cc, Hh, Ww = x.shape
            y0f = jnp.floor(py)
            x0f = jnp.floor(px)
            wy = (py - y0f).reshape(Bb, 1, -1)
            wx = (px - x0f).reshape(Bb, 1, -1)
            y0 = y0f.astype(jnp.int32)
            x0 = x0f.astype(jnp.int32)
            flat = x.reshape(Bb, Cc, Hh * Ww)

            def gather(yi, xi):
                valid = (yi >= 0) & (yi < Hh) & (xi >= 0) & (xi < Ww)
                yc = jnp.clip(yi, 0, Hh - 1)
                xc = jnp.clip(xi, 0, Ww - 1)
                idx = (yc * Ww + xc).reshape(Bb, 1, -1)
                g = jnp.take_along_axis(flat, jnp.broadcast_to(idx, (Bb, Cc, idx.shape[-1])), axis=2)
                return g * valid.reshape(Bb, 1, -1).astype(x.dtype)
            v00 = gather(y0, x0)
            v01 = gather(y0, x0 + 1)
            v10 = gather(y0 + 1, x0)
            v11 = gather(y0 + 1, x0 + 1)
            return v00 * (1 - wy) * (1 - wx) + v01 * (1 - wy) * wx + v10 * wy * (1 - wx) + v11 * wy * wx
        x = jax.nn.relu(x)
        offset = jax.lax.conv_general_dilated(x, w_off, (1, 1), ((1, 1), (1, 1)), dimension_numbers=('NCHW', 'OIHW', 'NCHW')) + b_off[None, :, None, None]
        Bb, Cc, Hh, Ww = x.shape
        Ho, Wo = (offset.shape[2], offset.shape[3])
        K2 = K * K
        off = offset.reshape(Bb, K2, 2, Ho, Wo)
        ky, kx = jnp.meshgrid(jnp.arange(K), jnp.arange(K), indexing='ij')
        ky = ky.reshape(-1).astype(x.dtype)
        kx = kx.reshape(-1).astype(x.dtype)
        base_y = jnp.arange(Ho, dtype=x.dtype)[None, :, None] - 1.0 + ky[:, None, None]
        base_x = jnp.arange(Wo, dtype=x.dtype)[None, None, :] - 1.0 + kx[:, None, None]
        py = base_y + off[:, :, 0]
        px = base_x + off[:, :, 1]
        samp = _bilinear_gather(x, py, px).reshape(Bb, Cc, K2, Ho, Wo)
        out = jnp.einsum('bckhw,ock->bohw', samp, w_def.reshape(w_def.shape[0], Cc, K2))
        return out

    def _gn(v, G=32, eps=1e-05):
        B_, C_, H_, W_ = v.shape
        g = v.reshape(B_, G, C_ // G, H_, W_)
        m = jnp.mean(g, axis=(2, 3, 4), keepdims=True)
        s = jnp.var(g, axis=(2, 3, 4), keepdims=True)
        return ((g - m) / jnp.sqrt(s + eps)).reshape(v.shape)

    def _ln_c(v, eps=1e-06):
        m = jnp.mean(v, axis=1, keepdims=True)
        s = jnp.var(v, axis=1, keepdims=True)
        return (v - m) / jnp.sqrt(s + eps)

    def _ln_t(v, eps=1e-05):
        m = jnp.mean(v, axis=-1, keepdims=True)
        s = jnp.var(v, axis=-1, keepdims=True)
        return (v - m) / jnp.sqrt(s + eps)

    def _to_tokens(v):
        B_, C_, H_, W_ = v.shape
        return v.reshape(B_, C_, H_ * W_).transpose(0, 2, 1)

    def _from_tokens(t, like):
        B_, C_, H_, W_ = like.shape
        return t.transpose(0, 2, 1).reshape(B_, C_, H_, W_)
    x = x + _L0_conv_ref(_gn(x), L0_conv_Wa, L0_conv_ba, L0_conv_Wb, L0_conv_bb, L0_conv_Wg, L0_conv_bg, L0_conv_Wo, L0_conv_bo)
    x = x + _L1_conv_ref(_gn(x), L1_conv_w_off, L1_conv_b_off, L1_conv_w_def)
    return x

_drawn_inputs = setup_inputs


def setup_inputs(seed=0):
    import zlib

    import numpy as np

    out = dict(_drawn_inputs(seed))
    spreads = {'L1_conv_b_off': (0.0, 0.1)}
    factors = {'L0_conv_bg': 3.142}
    for name, (base, spread) in spreads.items():
        noise = np.random.default_rng([zlib.crc32(name.encode()), seed]).standard_normal(out[name].shape)
        drawn = base * np.exp(spread * noise) if base else spread * noise
        out[name] = jnp.asarray(drawn.astype(out[name].dtype))
    for name, factor in factors.items():
        out[name] = (out[name] * factor).astype(out[name].dtype)
    return out
```

```python
from contextlib import ExitStack

import concourse.bass as bass
from concourse import mybir

IMGS, CH, HH, WW = 2, 128, 128, 128
P = 128
GC = 4
GROUPS = IMGS * CH // GC
GPI = CH // GC
FG = GC * WW
TAPS, NOFF = 9, 18

REACH = 2
MARGIN = REACH + 1
BR, WC = 4, 6
BPI = HH // BR
BANDS = IMGS * BPI
WINDOWS = -(-WW // WC)
LASTC = WW - (WINDOWS - 1) * WC
SRC_R, SRC_C = BR + 2 * MARGIN, WC + 2 * MARGIN
WPIX = SRC_R * SRC_C
PADR = HH + 2 * MARGIN
PADC = (WINDOWS - 1) * WC + SRC_C
BW = BR * WW
PAIRS = WINDOWS // 2
TGROUPS = -(-WINDOWS // 4)
BELOW_ALL = -1e30
EPS = 1e-5

ALU = mybir.AluOpType
ACT = mybir.ActivationFunctionType
AX = mybir.AxisListType
F32 = mybir.dt.float32
BF16 = mybir.dt.bfloat16
I32 = mybir.dt.int32

PART0, PART1, PART2, CONE = 0, 32, 64, 96
CROWS = 4
OFF_CHAIN = 9
BAND_STEPS, ROW_STEPS = 12, 2 + 4 * TAPS
FINAL_STEPS = 14
KROWS = CONE + CROWS


def wait(eng, sem, n):
    if isinstance(n, int) and n <= 0:
        return
    eng.wait_ge(sem, n)


def over(eng, first, last, end, step, body):
    for n in range(first):
        body(n, n % step)
    count = (end - first - last) // step * step
    with eng.Fori(0, count // step) as i:
        for u in range(step):
            body(i * step + (first + u), (first + u) % step)
    for n in range(first + count, end):
        body(n, n % step)


def preact_conv_kernel(nc, x, Wa, ba, Wb, bb, Wg, bg, Wo, bo, w_off, b_off, w_def,
                       ident_d, group_mask_d, select_d, select_all_d, coords_d, out):
    with ExitStack() as ctx:
        def sb(name, shape, dt=F32):
            return ctx.enter_context(nc.sbuf_tensor(name, shape, dt))

        def sem(name):
            return ctx.enter_context(nc.semaphore(name))

        x1_pad = nc.dram_tensor("x1_pad", [IMGS, CH, PADR, PADC], F32, kind="Internal").ap()

        pairs = [ctx.enter_context(nc.psum_tensor(f"pair{i}", [P, 2, 512], F32)) for i in range(2)]
        bank = [pairs[0][:, 0], pairs[0][:, 1], pairs[1][:, 0], pairs[1][:, 1]]
        bank += [ctx.enter_context(nc.psum_tensor(f"bank{i}", [P, 512], F32))[:]
                 for i in range(4, 8)]

        ident = sb("ident", [P, P])
        group_mask = sb("group_mask", [P, GPI])
        average = sb("average", [P, P])
        ones_row = sb("ones_row", [1, P])
        minus_half = sb("minus_half", [P, GROUPS])
        w_a, w_b, w_g, w_o = (sb(n, [P, P]) for n in ("w_a", "w_b", "w_g", "w_o"))
        bias_a, bias_g = sb("bias_a", [P, 1]), sb("bias_g", [P, 1])
        row_b, row_o = sb("row_b", [1, P]), sb("row_o", [1, P])
        all_b, all_o = sb("all_b", [P, P]), sb("all_o", [P, P])
        w_offs = sb("w_offs", [P, TAPS, NOFF])
        bias_off = sb("bias_off", [NOFF, 1])
        w_defs = sb("w_defs", [P, TAPS, P])
        select = sb("select", [P, NOFF, WPIX], BF16)

        XR = 4
        xg = sb("xg", [P, XR, FG])
        st6 = sb("st6", [P, XR, 6])
        mv = sb("mv", [P, XR, 2])
        mg = sb("mg", [P, XR, 2])
        dev = sb("dev", [P, XR])
        dev2 = sb("dev2", [P, XR])
        vare = sb("vare", [P, XR])
        rstd = sb("rstd", [P, XR])
        nbias = sb("nbias", [P, XR])
        xT = sb("xT", [P, FG])
        aT = sb("aT", [P, FG])
        gT = sb("gT", [P, FG])
        bm = sb("bm", [P, FG])
        gated = sb("gated", [P, FG])
        x_bo = sb("x_bo", [P, 2, FG])
        x1g = sb("x1g", [P, XR, GC, PADC])
        pad_rows = sb("pad_rows", [P, MARGIN * PADC])

        s6 = sb("s6", [P, 2, 6])
        mv1 = sb("mv1", [P, 2, 2])
        mv2 = sb("mv2", [P, GROUPS, 2])
        mg2 = sb("mg2", [P, GROUPS, 2])
        devs = sb("devs", [P, GROUPS])
        devs2 = sb("devs2", [P, GROUPS])
        vare2 = sb("vare2", [P, GROUPS])
        rstd2 = sb("rstd2", [P, GROUPS])
        nbias2 = sb("nbias2", [P, GROUPS])
        picked = sb("picked", [P, 2, IMGS, GPI])
        norm_c = sb("norm_c", [P, 2, IMGS])
        norm_band = sb("norm_band", [P, 2, IMGS, BPI])

        raw = sb("raw", [P, 2, SRC_R * PADC])
        z = sb("z", [P, 2, PADC, SRC_R])
        offs = sb("offs", [NOFF, BW])
        squares = sb("squares", [NOFF, BW])
        rest = sb("rest", [NOFF, BW])
        middle = sb("middle", [NOFF, BW], BF16)
        coords = sb("coords", [P, BW], BF16)
        farthest = sb("farthest", [NOFF, BANDS])
        dist = sb("dist", [WPIX, 2, 2, BW])
        hats = sb("hats", [WPIX, 2, 2, BW])
        weights = sb("weights", [WPIX, 2, TAPS, BW])
        zT = sb("zT", [WPIX, 2, WINDOWS, P])
        samples = sb("samples", [P, TAPS, BW])
        res = sb("res", [P, 2, BW])
        y = sb("y", [P, 2, BW])

        select_all = sb("select_all", [P, NOFF, P], BF16)
        far_band = sb("far_band", [BANDS, 1])
        far_any = sb("far_any", [1, 1])
        flags = sb("flags", [1, BANDS], I32)
        any_flag = sb("any_flag", [1, 1], I32)
        norm_now = sb("norm_now", [P, 2])
        band_row = sb("band_row", [P, 1])
        row_shift = sb("row_shift", [P, 1])
        row_in = sb("row_in", [P, WW])
        row_z = sb("row_z", [P, WW])
        row_zT = sb("row_zT", [P, P])
        far_dist = sb("far_dist", [P, 2, BW])
        far_hats = sb("far_hats", [P, 2, BW])
        far_weights = sb("far_weights", [P, BW])

        in_f32 = sem("in_f32")
        in_off = sem("in_off")
        in_def = sem("in_def")
        const_set = sem("const_set")
        rows_spread = sem("rows_spread")
        rows_copied = sem("rows_copied")
        x_in = [sem(f"x_in{s}") for s in range(XR)]
        x1_out = [sem(f"x1_out{s}") for s in range(XR)]
        pad_set = sem("pad_set")
        pad_out = sem("pad_out")
        bn_done = sem("bn_done")
        mv_ready = sem("mv_ready")
        mean_summed = sem("mean_summed")
        mg_ready = sem("mg_ready")
        dev_ready = sem("dev_ready")
        dev2_ready = sem("dev2_ready")
        var_summed = sem("var_summed")
        vare_ready = sem("vare_ready")
        rstd_ready = sem("rstd_ready")
        nb_ready = sem("nb_ready")
        x_turned = sem("x_turned")
        xT_ready = sem("xT_ready")
        a_done = sem("a_done")
        b_done = sem("b_done")
        g_done = sem("g_done")
        aT_ready = sem("aT_ready")
        bm_ready = sem("bm_ready")
        gT_ready = sem("gT_ready")
        ab_done = sem("ab_done")
        gated_ready = sem("gated_ready")
        o_done = sem("o_done")
        xbo_ready = sem("xbo_ready")
        x1_ready = sem("x1_ready")
        bn2_done = sem("bn2_done")
        mv1_ready = sem("mv1_ready")
        mv2_ready = sem("mv2_ready")
        final = sem("final")

        raw_in = [sem(f"raw_in{s}") for s in range(2)]
        res_in = [sem(f"res_in{s}") for s in range(2)]
        z_ready = sem("z_ready")
        off_done = sem("off_done")
        off_biased = sem("off_biased")
        off_chain = sem("off_chain")
        coords_ready = sem("coords_ready")
        coord_done = sem("coord_done")
        dist_ready = sem("dist_ready")
        hats_ready = sem("hats_ready")
        weights_ready = sem("weights_ready")
        z_turned = sem("z_turned")
        zT_a = sem("zT_a")
        zT_v = sem("zT_v")
        sampled = sem("sampled")
        samples_ready = sem("samples_ready")
        conv_done = sem("conv_done")
        y_ready = sem("y_ready")
        y_out = [sem(f"y_out{s}") for s in range(2)]

        far_step = sem("far_step")
        flags_ready = sem("flags_ready")
        waits_taken = sem("waits_taken")
        band_row_set = sem("band_row_set")
        g_raw_in, g_row_in, g_res_in, g_y_out = (sem(f"g_{n}") for n in ("raw_in", "row_in",
                                                                         "res_in", "y_out"))
        g_off_done, g_row_turned, g_coord_done, g_sampled, g_conv_done = (
            sem(f"g_{n}") for n in ("off_done", "row_turned", "coord_done", "sampled", "conv_done"))
        g_step, g_z_ready, g_coords_ready, g_row_ready, g_zT_ready = (
            sem(f"g_{n}") for n in ("step", "z_ready", "coords_ready", "row_ready", "zT_ready"))
        g_weights_ready, g_added, g_y_ready = (
            sem(f"g_{n}") for n in ("weights_ready", "added", "y_ready"))

        def after_wait(eng):
            eng.sem_inc(waits_taken, 1)

        def general(eng, band, per_band, at_start=None, before_image=None, before_band=None):
            eng.wait_ge(flags_ready, 2)
            needed = eng.value_load(any_flag[:], min_val=0, max_val=1)
            with eng.If(needed != 0):
                if at_start:
                    at_start()
                with eng.Fori(0, IMGS) as img:
                    if before_image:
                        before_image()
                    with eng.Fori(0, BPI) as b:
                        n = img * BPI + b
                        if before_band:
                            before_band(img, n)
                        flag = eng.value_load(flags[0:1, bass.ds(n, 1)], min_val=0, max_val=1)
                        with eng.If(flag != 0):
                            band(img, b, n)
                        with eng.Else():
                            for semaphore, count in per_band:
                                eng.sem_inc(semaphore, count)

        x_groups = x.rearrange("b (g f) h w -> (b g) h f w", f=GC)
        x1_groups = x1_pad.rearrange("b (g f) r w -> (b g) r f w", f=GC)
        out_v = out.rearrange("b c h w -> b c (h w)")

        B_T, B_A, B_B, B_G, B_AB, B_O, B_ST = range(7)
        B_ZT, B_S = (4, 5), (6, 7)
        B_OFF, B_CONV = B_ZT

        def zT_copied(n, g):
            a = sum(1 for h in range(g + 1) if h % 2 == 0)
            v = g + 1 - a
            na = (TGROUPS + 1) // 2
            return n * na + a, n * (TGROUPS - na) + v

        ORDER = [(step[0], int(step[1:])) for step in (
            "c0 c1 c2 c3 k0 c4 c5 k1 c6 c7 k2 c8 k3 s0 T0 s1 k4 s2 T1 s3 k5 s4 T2 k6 s5 T3 s6 k7 "
            "s7 T4 k8 s8 T5 s9 O0 s10").split()]

        def bands(eng, stages, prologue):
            prologue()

            def band(n, u):
                for kind, j in ORDER:
                    ahead = {"c": -1, "k": 1, "s": 0, "T": 1, "O": 2}[kind]
                    if isinstance(n, int) and not 0 <= n + ahead < BANDS:
                        continue
                    if kind in stages:
                        stages[kind](n + ahead, (u + ahead) % 2, j)

            over(eng, 3, 4, BANDS + 1, 2, band)

        block = ctx.enter_context(nc.Block())

        @block.sync
        def _(sp):
            def load_x(g, s):
                wait(sp, x_turned, g - XR + 1)
                wait(sp, xbo_ready, g - XR + 1)
                sp.dma_start(xg[:, s, :].rearrange("p (f w) -> p f w", f=GC),
                             x_groups[bass.ds(g, 1)].rearrange("g h f w -> (g h) f w")
                             ).then_inc(x_in[s], 16)

            for g in range(2):
                load_x(g, g)
            for dst, src in ((w_a[:], Wa), (w_b[:], Wb), (w_g[:], Wg), (w_o[:], Wo),
                             (bias_a[:], ba.rearrange("(p a) -> p a", a=1)),
                             (bias_g[:], bg.rearrange("(p a) -> p a", a=1)),
                             (row_b[:], bb.rearrange("(a p) -> a p", a=1)),
                             (row_o[:], bo.rearrange("(a p) -> a p", a=1)),
                             (ident[:], ident_d), (group_mask[:], group_mask_d)):
                sp.dma_start(dst, src).then_inc(in_f32, 16)
            for g in range(2, XR):
                load_x(g, g)
            for dst, src in ((w_offs[:], w_off), (bias_off[:], b_off.rearrange("(p a) -> p a", a=1)),
                             (select[:], select_d)):
                sp.dma_start(dst, src).then_inc(in_off, 16)
            sp.wait_ge(const_set, 6)
            sp.dma_start(coords[CONE:KROWS, :], coords_d).then_inc(in_off, 16)
            sp.dma_start(w_defs[:], w_def).then_inc(in_def, 16)
            sp.dma_start(select_all[:], select_all_d).then_inc(in_def, 16)
            sp.wait_ge(pad_set, 1)
            for b in range(IMGS):
                for r in (0, PADR - MARGIN):
                    sp.dma_start(x1_pad[b, :, r:r + MARGIN, :].rearrange("c r w -> c (r w)"),
                                 pad_rows[:]).then_inc(pad_out, 16)

            def store_x1(g, s):
                wait(sp, x1_ready, g + 1)
                sp.dma_start(x1_groups[bass.ds(g, 1), MARGIN:MARGIN + HH]
                             .rearrange("g r f w -> (g r) f w"),
                             x1g[:, s]).then_inc(x1_out[s], 16)

            def group(g, s):
                if not isinstance(g, int) or g + XR < GROUPS:
                    load_x(g + XR, s)
                if not isinstance(g, int) or g > 0:
                    store_x1(g - 1, (s - 1) % XR)

            over(sp, 1, XR, GROUPS, XR, group)
            store_x1(GROUPS - 1, (GROUPS - 1) % XR)

            for s in range(XR):
                sp.wait_ge(x1_out[s], 16 * GROUPS // XR)
            sp.wait_ge(pad_out, 16 * 2 * IMGS)

            def load_raw(n, s):
                wait(sp, z_ready, n - 1)
                sp.dma_start(raw[:, s, :],
                             x1_pad[bass.ds(n // BPI, 1), :, bass.ds(n % BPI * BR, SRC_R), :]
                             .rearrange("b c r w -> (b c) (r w)")).then_inc(raw_in[s], 16)

            def load_res(n, s):
                wait(sp, y_ready, n - 1)
                sp.dma_start(res[:, s, :].rearrange("p (r w) -> p r w", r=BR),
                             x1_pad[bass.ds(n // BPI, 1), :, bass.ds(n % BPI * BR + MARGIN, BR),
                                    MARGIN:MARGIN + WW]
                             .rearrange("b c r w -> (b c) r w")).then_inc(res_in[s], 16)

            def store_y(n, s):
                wait(sp, y_ready, n + 1)
                sp.dma_start(out_v[bass.ds(n // BPI, 1), :, bass.ds(n % BPI * BW, BW)]
                             .rearrange("b c q -> (b c) q"), y[:, s, :]).then_inc(y_out[s], 16)

            load_raw(0, 0)
            load_raw(1, 1)

            def band(n, s):
                known = isinstance(n, int)
                if not known or n + 2 < BANDS:
                    load_raw(n + 2, s)
                if not known or n < BANDS:
                    load_res(n, s)
                if not known or n >= 2:
                    store_y(n - 2, s)

            over(sp, 2, 4, BANDS + 2, 2, band)
            for s in range(2):
                sp.wait_ge(y_out[s], 16 * BANDS // 2)

            def far_band_io(img, b, n):
                sp.dma_start(raw[:, 0, :], x1_pad[bass.ds(img, 1), :, bass.ds(b * BR, SRC_R), :]
                             .rearrange("b c r w -> (b c) (r w)")).then_inc(g_raw_in, 16)
                sp.dma_start(res[:, 0, :].rearrange("p (r w) -> p r w", r=BR),
                             x1_pad[bass.ds(img, 1), :, bass.ds(b * BR + MARGIN, BR),
                                    MARGIN:MARGIN + WW]
                             .rearrange("b c r w -> (b c) r w")).then_inc(g_res_in, 16)
                with sp.Fori(0, HH) as h:
                    sp.wait_ge(g_row_ready, n * HH + h + 1)
                    sp.dma_start(row_in[:], x1_pad[bass.ds(img, 1), :, bass.ds(h + MARGIN, 1),
                                                   MARGIN:MARGIN + WW]
                                 .rearrange("b c r w -> (b c) (r w)")).then_inc(g_row_in, 16)
                sp.wait_ge(g_y_ready, n + 1)
                sp.dma_start(out_v[bass.ds(img, 1), :, bass.ds(b * BW, BW)]
                             .rearrange("b c q -> (b c) q"), y[:, 0, :]).then_inc(g_y_out, 16)
                sp.wait_ge(g_y_out, 16 * n + 16)
                after_wait(sp)

            general(sp, far_band_io, ((g_raw_in, 16), (g_res_in, 16), (g_row_in, 16 * HH),
                                      (g_y_out, 16)))

        @block.tensor
        def _(pe):
            pe.wait_ge(in_f32, 160)
            pe.wait_ge(const_set, 2)
            nc.tensor.matmul(bank[B_B][:, 0:P], ones_row[:], row_b[:], start=True, stop=True)
            nc.tensor.matmul(bank[B_B][:, P:2 * P], ones_row[:], row_o[:], start=True,
                             stop=True).then_inc(rows_spread, 1)

            def mean_sum(g, s):
                wait(pe, mv_ready, g + 1)
                wait(pe, vare_ready, g)
                nc.tensor.matmul(bank[B_ST][:, 0:2], average[:], mv[:, s, :], start=True,
                                 stop=True).then_inc(mean_summed, 1)

            def var_sum(g, s):
                wait(pe, dev2_ready, g + 1)
                nc.tensor.matmul(bank[B_ST][:, 2:3], average[:], dev2[:, s:s + 1], start=True,
                                 stop=True).then_inc(var_summed, 1)

            def turn(g, s):
                wait(pe, xT_ready, g)
                if isinstance(g, int):
                    pe.wait_ge(x_in[s], 16 * (g // XR + 1))
                else:
                    pe.wait_ge(x_in[s], (g - s) * (16 // XR) + 16)
                for f in range(GC):
                    mm = nc.tensor.transpose(bank[B_T][:, f * P:(f + 1) * P],
                                             xg[:, s, f * WW:(f + 1) * WW], ident[:])
                mm.then_inc(x_turned, 1)

            def gate(g):
                wait(pe, gated_ready, g + 1)
                wait(pe, x1_ready, g)
                for f in range(GC):
                    mm = nc.tensor.matmul(bank[B_O][:, f * P:(f + 1) * P],
                                          gated[:, f * P:(f + 1) * P], w_o[:],
                                          start=True, stop=True)
                mm.then_inc(o_done, 1)

            def stats_ahead(g):
                return not isinstance(g, int) or g + 2 < GROUPS

            mean_sum(0, 0)
            var_sum(0, 0)
            mean_sum(1, 1)
            var_sum(1, 1)
            turn(0, 0)

            def group(g, s):
                known = isinstance(g, int)
                pe.wait_ge(xT_ready, g + 1)
                wait(pe, aT_ready, g)
                nc.tensor.matmul(bank[B_A], w_a[:], xT[:], start=True,
                                 stop=True).then_inc(a_done, 1)
                wait(pe, bm_ready, g)
                if known and g == 0:
                    pe.wait_ge(rows_copied, 1)
                for f in range(GC):
                    mm = nc.tensor.matmul(bank[B_B][:, f * P:(f + 1) * P],
                                          xT[:, f * P:(f + 1) * P], w_b[:], start=True, stop=True)
                mm.then_inc(b_done, 1)
                wait(pe, gT_ready, g)
                nc.tensor.matmul(bank[B_G], w_g[:], xT[:], start=True,
                                 stop=True).then_inc(g_done, 1)
                if stats_ahead(g):
                    mean_sum(g + 2, (s + 2) % XR)
                if not known or g > 0:
                    gate(g - 1)
                if stats_ahead(g):
                    var_sum(g + 2, (s + 2) % XR)
                if not known or g + 1 < GROUPS:
                    turn(g + 1, (s + 1) % XR)
                pe.wait_ge(aT_ready, g + 1)
                pe.wait_ge(bm_ready, g + 1)
                wait(pe, gated_ready, g)
                for f in range(GC):
                    mm = nc.tensor.matmul(bank[B_AB][:, f * P:(f + 1) * P],
                                          bm[:, f * P:(f + 1) * P], aT[:, f * P:(f + 1) * P],
                                          start=True, stop=True)
                mm.then_inc(ab_done, 1)

            over(pe, 2, 2, GROUPS, XR, group)
            gate(GROUPS - 1)

            pe.wait_ge(mv2_ready, GROUPS)
            nc.tensor.matmul(bank[B_ST][:, 0:2 * GROUPS], average[:],
                             mv2[:].rearrange("p g k -> p (g k)"), start=True,
                             stop=True).then_inc(final, 1)
            pe.wait_ge(final, 4)
            nc.tensor.matmul(bank[B_ST][:, 2 * GROUPS:3 * GROUPS], average[:], devs2[:],
                             start=True, stop=True).then_inc(final, 1)

            def conv(n, u, k):
                if k == 0:
                    wait(pe, samples_ready, PAIRS * (n + 1) )
                    wait(pe, y_ready, n)
                    a, v = zT_copied(n + 1, TGROUPS - 1)
                    if not isinstance(n, int):
                        pe.wait_ge(zT_v, v)
                    elif n + 1 < BANDS:
                        pe.wait_ge(zT_v, v)
                mm = nc.tensor.matmul(bank[B_CONV], w_defs[:, k, :],
                                      samples[:, k, :],
                                      start=(k == 0), stop=(k == TAPS - 1))
                if k == TAPS - 1:
                    mm.then_inc(conv_done, 1)

            def coordinates(n, u, k):
                b = (TAPS * u + k) % 2
                if k == 0:
                    wait(pe, coords_ready, n + 1)
                wait(pe, dist_ready, TAPS * n + k - 1)
                for d in range(2):
                    mm = nc.tensor.matmul(pairs[b][0:WPIX, d, :], select[0:KROWS, 2 * k + d, :],
                                          coords[0:KROWS, :], start=True, stop=True)
                mm.then_inc(coord_done, 1)

            def sample(n, u, p):
                b = (PAIRS * u + p) % 2
                if p == 0:
                    wait(pe, weights_ready, TAPS * (n + 1))
                    a, v = zT_copied(n, TGROUPS - 1)
                    pe.wait_ge(zT_a, a)
                    pe.wait_ge(zT_v, v)
                wait(pe, samples_ready, PAIRS * n + p - 1)
                for w in (2 * p, 2 * p + 1):
                    cols = min(WC, WW - w * WC)
                    at = (w % 2) * TAPS * BR * WC
                    mm = nc.tensor.matmul(
                        bank[B_S[b]][:, at:at + TAPS * BR * cols]
                        .rearrange("p (k c) -> p k c", k=TAPS),
                        zT[:, u, w, :],
                        weights[:, u, :, w * WC * BR:(w * WC + cols) * BR],
                        start=True, stop=True)
                mm.then_inc(sampled, 1)

            def turn_windows(n, u, g):
                if g == 0:
                    wait(pe, z_ready, n + 1)
                    pe.wait_ge(off_biased, n + 1)
                    pe.wait_ge(off_chain, OFF_CHAIN * n + 3)
                elif g == 1:
                    wait(pe, y_ready, n - 1)
                else:
                    a, v = zT_copied(n, g - 2)
                    pe.wait_ge(*((zT_a, a) if g % 2 == 0 else (zT_v, v)))
                ws = range(4 * g, min(4 * g + 4, WINDOWS))
                for w in ws:
                    mm = nc.tensor.transpose(
                        bank[B_ZT[g % 2]][0:WPIX, (w % 4) * P:(w % 4 + 1) * P],
                        z[:, u, w * WC:w * WC + SRC_C, :].rearrange("p w r -> p (w r)"),
                        ident[:])
                mm.then_inc(z_turned, 1)

            def convolve_offsets(u):
                q = 4
                for k in range(TAPS):
                    ky, kx = k // 3, k % 3
                    at = 32 * (k % q)
                    mm = nc.tensor.matmul(
                        bank[B_OFF][at:at + NOFF, :].rearrange("p (w r) -> p w r", r=BR),
                        w_offs[:, k, :],
                        z[:, u, MARGIN - 1 + kx:MARGIN - 1 + kx + WW,
                          MARGIN - 1 + ky:MARGIN - 1 + ky + BR],
                        start=(k < q), stop=(k + q >= TAPS), tile_position=(0, at))
                return mm

            def offsets(n, u, _):
                wait(pe, z_ready, n + 1)
                if not isinstance(n, int) or n > 0:
                    pe.wait_ge(zT_a, zT_copied(n - 1, TGROUPS - 2)[0])
                convolve_offsets(u).then_inc(off_done, 1)

            def prologue():
                pe.wait_ge(in_off, 64)
                offsets(0, 0, 0)
                for k in range(TAPS):
                    coordinates(0, 0, k)
                for g in range(TGROUPS):
                    turn_windows(0, 0, g)
                offsets(1, 1, 0)
                pe.wait_ge(in_def, 32)

            bands(pe, {"c": conv, "k": coordinates, "s": sample, "T": turn_windows,
                       "O": offsets}, prologue)

            pe.wait_ge(far_step, 1)
            nc.tensor.transpose(bank[B_OFF][0:BANDS, 0:NOFF], farthest[:],
                                ident[0:NOFF, 0:NOFF]).then_inc(far_step, 1)
            pe.wait_ge(far_step, 3)
            nc.tensor.transpose(bank[B_OFF][0:1, 0:BANDS], far_band[:],
                                ident[0:BANDS, 0:BANDS]).then_inc(far_step, 1)

            def far_band_products(img, b, n):
                pe.wait_ge(g_z_ready, n + 1)
                convolve_offsets(0).then_inc(g_off_done, 1)
                pe.wait_ge(g_coords_ready, n + 1)
                after_wait(pe)
                with pe.Fori(0, HH) as h:
                    row = n * HH + h
                    pe.wait_ge(g_row_ready, row + 2)
                    nc.tensor.transpose(bank[B_CONV][:, 0:P], row_z[:],
                                        ident[:]).then_inc(g_row_turned, 1)
                    for k in range(TAPS):
                        for d in range(2):
                            mm = nc.tensor.matmul(pairs[0][:, d, :],
                                                  select_all[0:KROWS, 2 * k + d, :],
                                                  coords[0:KROWS, :], start=True, stop=True)
                        mm.then_inc(g_coord_done, 1)
                        if k == 0:
                            pe.wait_ge(g_zT_ready, row + 1)
                        pe.wait_ge(g_weights_ready, row * TAPS + k + 1)
                        nc.tensor.matmul(bank[B_S[0]], row_zT[:], far_weights[:], start=True,
                                         stop=True).then_inc(g_sampled, 1)
                pe.wait_ge(g_added, (n + 1) * HH * TAPS)
                for k in range(TAPS):
                    mm = nc.tensor.matmul(bank[B_CONV], w_defs[:, k, :], samples[:, k, :],
                                          start=(k == 0), stop=(k == TAPS - 1))
                mm.then_inc(g_conv_done, 1)
                pe.wait_ge(g_conv_done, n + 1)
                after_wait(pe)

            general(pe, far_band_products,
                    ((g_off_done, 1), (g_row_turned, HH), (g_coord_done, HH * TAPS),
                     (g_sampled, HH * TAPS), (g_conv_done, 1)))

        @block.scalar
        def _(act):
            act.wait_ge(in_f32, 160)

            def norm_x(g, s):
                pe_done = g + 1
                wait(act, x_turned, pe_done)
                wait(act, nb_ready, g + 1)
                wait(act, g_done, g)
                nc.scalar.activation(xT[:], bank[B_T], ACT.Identity,
                                     bias=nbias[:, s:s + 1],
                                     scale=rstd[:, s:s + 1]).then_inc(xT_ready, 1)

            norm_x(0, 0)

            def group(g, s):
                act.wait_ge(a_done, g + 1)
                wait(act, ab_done, g)
                nc.scalar.activation(aT[:], bank[B_A], ACT.Identity,
                                     bias=bias_a[:]).then_inc(aT_ready, 1)
                act.wait_ge(g_done, g + 1)
                wait(act, gated_ready, g)
                nc.scalar.activation(gT[:], bank[B_G], ACT.Sigmoid,
                                     bias=bias_g[:]).then_inc(gT_ready, 1)
                if not isinstance(g, int) or g + 1 < GROUPS:
                    norm_x(g + 1, (s + 1) % XR)

            over(act, 1, 3, GROUPS, XR, group)

            def make_z(n, u):
                if isinstance(n, int):
                    act.wait_ge(raw_in[u], 16 * (n // 2 + 1))
                else:
                    act.wait_ge(raw_in[u], (n - u) * 8 + 16)
                a, v = zT_copied(n - 2, TGROUPS - 1)
                wait(act, z_turned, TGROUPS * (n - 1))
                wait(act, off_done, n - 1)
                nc.scalar.activation(
                    z[:, u], raw[:, u, :].rearrange("p (r w) -> p w r", r=SRC_R), ACT.Relu,
                    bias=norm_band[:, 1].rearrange("p b n -> p (b n)")[:, bass.ds(n, 1)],
                    scale=norm_band[:, 0].rearrange("p b n -> p (b n)")[:, bass.ds(n, 1)]
                ).then_inc(z_ready, 1)

            def bias_offsets(n, u, _):
                act.wait_ge(off_done, n + 1)
                wait(act, off_chain, OFF_CHAIN * n)
                nc.scalar.activation(offs[:], bank[B_OFF][0:NOFF, :], ACT.Identity,
                                     bias=bias_off[:]).then_inc(off_biased, 1)

            def distances(n, u, k):
                b = (TAPS * u + k) % 2
                t = TAPS * n + k
                act.wait_ge(coord_done, t + 1)
                wait(act, hats_ready, t - 1)
                nc.scalar.activation(dist[:, b], pairs[b][0:WPIX], ACT.Abs).then_inc(dist_ready, 1)

            def copy_samples(n, u, p):
                b = (PAIRS * u + p) % 2
                wait(act, sampled, PAIRS * n + p + 1)
                if p == 0:
                    wait(act, conv_done, n)
                wc = WC * BR
                if p < PAIRS - 1:
                    nc.scalar.copy(
                        samples[:, :, 2 * p * wc:2 * (p + 1) * wc]
                        .rearrange("p k (w c) -> p w k c", w=2),
                        bank[B_S[b]][:, 0:2 * TAPS * wc]
                        .rearrange("p (w k c) -> p w k c", w=2, c=wc)).then_inc(samples_ready, 1)
                else:
                    nc.scalar.copy(
                        samples[:, :, 2 * p * wc:(2 * p + 1) * wc],
                        bank[B_S[b]][:, 0:TAPS * wc].rearrange("p (k c) -> p k c", c=wc))
                    nc.scalar.copy(
                        samples[:, :, (WW - LASTC) * BR:BW],
                        bank[B_S[b]][:, TAPS * wc:TAPS * (wc + LASTC * BR)]
                        .rearrange("p (k c) -> p k c", k=TAPS)).then_inc(samples_ready, 1)

            def copy_windows(n, u, g):
                if g % 2:
                    return
                wait(act, z_turned, TGROUPS * n + g + 1)
                if g == 0:
                    wait(act, sampled, PAIRS * (n - 1))
                c = min(4, WINDOWS - 4 * g)
                nc.scalar.copy(zT[:, u, 4 * g:4 * g + c, :].rearrange("p w c -> p (w c)"),
                               bank[B_ZT[0]][0:WPIX, 0:c * P]).then_inc(zT_a, 1)

            def with_z(n, u, k):
                distances(n, u, k)
                if k == 1 and (not isinstance(n, int) or n + 1 < BANDS):
                    make_z(n + 1, (u + 1) % 2)

            def prologue():
                act.wait_ge(in_off, 64)
                act.wait_ge(final, FINAL_STEPS)
                make_z(0, 0)
                make_z(1, 1)
                bias_offsets(0, 0, 0)
                for k in range(TAPS):
                    distances(0, 0, k)
                for g in range(TGROUPS):
                    copy_windows(0, 0, g)
                bias_offsets(1, 1, 0)

            bands(act, {"k": with_z, "s": copy_samples, "T": copy_windows, "O": bias_offsets},
                  prologue)

        @block.vector
        def _(dve):
            nc.vector.memset(average[:], 1.0 / P).then_inc(const_set, 1)
            nc.vector.memset(ones_row[:], 1.0).then_inc(const_set, 1)
            nc.vector.memset(coords[0:64, :], 0.0).then_inc(const_set, 1)
            nc.vector.memset(coords[64:128, :], 0.0).then_inc(const_set, 1)
            nc.vector.memset(minus_half[:], -0.5).then_inc(const_set, 1)
            nc.vector.memset(x1g[:], BELOW_ALL).then_inc(const_set, 1)
            nc.vector.memset(pad_rows[:], BELOW_ALL).then_inc(pad_set, 1)

            dve.wait_ge(rows_spread, 1)
            nc.vector.tensor_copy(all_b[:], bank[B_B][:, 0:P])
            nc.vector.tensor_copy(all_o[:], bank[B_B][:, P:2 * P]).then_inc(rows_copied, 1)
            dve.wait_ge(rows_copied, 1)
            dve.wait_ge(const_set, 6)

            def row_stats(g, s):
                if isinstance(g, int):
                    dve.wait_ge(x_in[s], 16 * (g // XR + 1))
                else:
                    dve.wait_ge(x_in[s], (g - s) * (16 // XR) + 16)
                nc.vector.bn_stats(st6[:, s, :], xg[:, s, :]).then_inc(bn_done, 1)

            def row_means(g, s):
                nc.vector.bn_aggr(mv[:, s, :], st6[:, s, :]).then_inc(mv_ready, 1)

            def deviations(g, s):
                dve.wait_ge(mean_summed, g + 1)
                nc.vector.tensor_copy(mg[:, s, :], bank[B_ST][:, 0:2]).then_inc(mg_ready, 1)
                dve.wait_ge(mg_ready, g + 1)
                nc.vector.tensor_tensor(dev[:, s:s + 1], mv[:, s, 0:1], mg[:, s, 0:1],
                                        ALU.subtract).then_inc(dev_ready, 1)
                dve.wait_ge(dev_ready, g + 1)
                nc.vector.tensor_tensor(dev2[:, s:s + 1], dev[:, s:s + 1], dev[:, s:s + 1],
                                        ALU.mult).then_inc(dev2_ready, 1)

            def variance(g, s):
                dve.wait_ge(var_summed, g + 1)
                nc.vector.scalar_tensor_tensor(
                    out=vare[:, s:s + 1], in0=bank[B_ST][:, 2:3], scalar=EPS,
                    in1=mg[:, s, 1:2], op0=ALU.add, op1=ALU.add).then_inc(vare_ready, 1)

            def norm_bias(g, s):
                dve.wait_ge(rstd_ready, g + 1)
                nc.vector.scalar_tensor_tensor(
                    out=nbias[:, s:s + 1], in0=mg[:, s, 0:1], scalar=-1.0,
                    in1=rstd[:, s:s + 1], op0=ALU.mult, op1=ALU.mult).then_inc(nb_ready, 1)

            def add_x(g, s):
                dve.wait_ge(o_done, g + 1)
                wait(dve, xbo_ready, g + 1)
                if isinstance(g, int):
                    wait(dve, x1_out[s], 16 * (g // XR))
                else:
                    dve.wait_ge(x1_out[s], (g - s) * (16 // XR))
                h = x1g[:, s, :, MARGIN:MARGIN + WW]
                nc.vector.tensor_tensor(
                    h, bank[B_O].rearrange("p (f w) -> p f w", f=GC),
                    x_bo[:, s % 2, :].rearrange("p (f w) -> p f w", f=GC),
                    ALU.add).then_inc(x1_ready, 1)
                dve.wait_ge(x1_ready, g + 1)
                nc.vector.bn_stats(s6[:, s % 2, :], h).then_inc(bn2_done, 1)

            def x1_means(g, s):
                nc.vector.bn_aggr(mv1[:, s % 2, :], s6[:, s % 2, :]).then_inc(mv1_ready, 1)

            def keep_x1_means(g, s):
                dve.wait_ge(mv1_ready, g + 1)
                nc.vector.tensor_copy(mv2[:, bass.ds(g, 1), :].rearrange("p g k -> p (g k)"),
                                      mv1[:, s % 2, :]).then_inc(mv2_ready, 1)

            for g in range(2):
                row_stats(g, g)
                dve.wait_ge(bn_done, g + 1)
                row_means(g, g)
                deviations(g, g)
                variance(g, g)
                norm_bias(g, g)

            def group(g, s):
                known = isinstance(g, int)
                ahead = not known or g + 2 < GROUPS
                t = (s + 2) % XR
                if ahead:
                    row_stats(g + 2, t)
                dve.wait_ge(b_done, g + 1)
                wait(dve, ab_done, g)
                if ahead:
                    dve.wait_ge(bn_done, g + 3)
                nc.vector.tensor_tensor(
                    bm[:].rearrange("p (f l) -> p f l", f=GC),
                    bank[B_B].rearrange("p (f l) -> p f l", f=GC),
                    all_b[:].rearrange("p (f l) -> p f l", f=1).broadcast_to([P, GC, P]),
                    ALU.add).then_inc(bm_ready, 1)
                if ahead:
                    row_means(g + 2, t)
                    deviations(g + 2, t)
                behind = not known or g > 0
                if behind:
                    add_x(g - 1, (s - 1) % XR)
                    dve.wait_ge(bn2_done, g)
                if ahead:
                    variance(g + 2, t)
                if behind:
                    x1_means(g - 1, (s - 1) % XR)
                if ahead:
                    norm_bias(g + 2, t)
                if behind:
                    keep_x1_means(g - 1, (s - 1) % XR)
                dve.wait_ge(ab_done, g + 1)
                dve.wait_ge(gT_ready, g + 1)
                wait(dve, o_done, g)
                nc.vector.tensor_tensor(gated[:], bank[B_AB], gT[:],
                                        ALU.mult).then_inc(gated_ready, 1)

            over(dve, 1 + XR, 3, GROUPS, XR, group)
            last = (GROUPS - 1, (GROUPS - 1) % XR)
            add_x(*last)
            dve.wait_ge(bn2_done, GROUPS)
            x1_means(*last)
            keep_x1_means(*last)

            dve.wait_ge(final, 1)
            nc.vector.tensor_copy(mg2[:].rearrange("p g k -> p (g k)"),
                                  bank[B_ST][:, 0:2 * GROUPS]).then_inc(final, 1)
            dve.wait_ge(final, 2)
            nc.vector.tensor_tensor(devs[:], mv2[:, :, 0], mg2[:, :, 0],
                                    ALU.subtract).then_inc(final, 1)
            dve.wait_ge(final, 3)
            nc.vector.tensor_tensor(devs2[:], devs[:], devs[:], ALU.mult).then_inc(final, 1)
            dve.wait_ge(final, 5)
            nc.vector.scalar_tensor_tensor(
                out=vare2[:], in0=bank[B_ST][:, 2 * GROUPS:3 * GROUPS], scalar=EPS,
                in1=mg2[:, :, 1], op0=ALU.add, op1=ALU.add).then_inc(final, 1)
            dve.wait_ge(final, 7)
            nc.vector.scalar_tensor_tensor(
                out=nbias2[:], in0=mg2[:, :, 0], scalar=-1.0, in1=rstd2[:],
                op0=ALU.mult, op1=ALU.mult).then_inc(final, 1)
            dve.wait_ge(final, 8)
            for j, per_group in enumerate((rstd2, nbias2)):
                nc.vector.tensor_tensor(
                    picked[:, j], per_group[:].rearrange("p (b g) -> p b g", b=IMGS),
                    group_mask[:].rearrange("p (b g) -> p b g", b=1)
                    .broadcast_to([P, IMGS, GPI]), ALU.mult).then_inc(final, 1)
            dve.wait_ge(final, 10)
            for j in range(2):
                nc.vector.tensor_reduce(norm_c[:, j, :], picked[:, j], AX.X,
                                        ALU.add).then_inc(final, 1)
            dve.wait_ge(final, 12)
            for j in range(2):
                nc.vector.tensor_copy(
                    norm_band[:, j],
                    norm_c[:, j, :].rearrange("p (b n) -> p b n", n=1)
                    .broadcast_to([P, IMGS, BPI])).then_inc(final, 1)

            def make_hats(n, u, k):
                b = (TAPS * u + k) % 2
                t = TAPS * n + k
                dve.wait_ge(dist_ready, t + 1)
                wait(dve, weights_ready, t - 1)
                nc.vector.tensor_scalar(hats[:, b], dist[:, b], -1.0, 0.0, ALU.add,
                                        ALU.min).then_inc(hats_ready, 1)

            def weigh(n, u, k):
                b = (TAPS * u + k) % 2
                t = TAPS * n + k
                dve.wait_ge(hats_ready, t + 1)
                if k == 0:
                    wait(dve, sampled, PAIRS * (n - 1))
                nc.vector.tensor_tensor(weights[:, u, k, :], hats[:, b, 0, :], hats[:, b, 1, :],
                                        ALU.mult).then_inc(weights_ready, 1)

            def taps(n, u, k):
                make_hats(n, u, k)
                weigh(n, u, k)

            def split_offsets(n, u, _):
                c = OFF_CHAIN * n

                def done(ins, j):
                    ins.then_inc(off_chain, 1)
                    dve.wait_ge(off_chain, c + j)

                dve.wait_ge(off_biased, n + 1)
                for j in (1, 2, 3):
                    done(nc.vector.tensor_tensor(
                        offs[:], bank[B_OFF][32 * j:32 * j + NOFF, :], offs[:], ALU.add), j)
                done(nc.vector.tensor_tensor(squares[:], offs[:], offs[:], ALU.mult), 4)
                wait(dve, coord_done, TAPS * n)
                done(nc.vector.tensor_copy(coords[PART0:PART0 + NOFF, :], offs[:]), 5)
                done(nc.vector.tensor_tensor(rest[:], offs[:], coords[PART0:PART0 + NOFF, :],
                                             ALU.subtract), 6)
                done(nc.vector.tensor_copy(middle[:], rest[:]), 7)
                done(nc.vector.tensor_tensor(coords[PART2:PART2 + NOFF, :], rest[:], middle[:],
                                             ALU.subtract), 8)
                nc.vector.tensor_copy(coords[PART1:PART1 + NOFF, :],
                                      middle[:]).then_inc(coords_ready, 1)
                nc.vector.tensor_reduce(farthest[:, bass.ds(n, 1)], squares[:], AX.X,
                                        ALU.max).then_inc(off_chain, 1)

            def copy_windows(n, u, g):
                if g % 2 == 0:
                    return
                dve.wait_ge(z_turned, TGROUPS * n + g + 1)
                if g == 1:
                    wait(dve, sampled, PAIRS * (n - 1))
                c = min(4, WINDOWS - 4 * g)
                nc.vector.tensor_copy(zT[:, u, 4 * g:4 * g + c, :].rearrange("p w c -> p (w c)"),
                                      bank[B_ZT[1]][0:WPIX, 0:c * P]).then_inc(zT_v, 1)

            def add_x1(n, u, k):
                if k < TAPS - 1:
                    return
                dve.wait_ge(conv_done, n + 1)
                if isinstance(n, int):
                    dve.wait_ge(res_in[u], 16 * (n // 2 + 1))
                    wait(dve, y_out[u], 16 * (n // 2))
                else:
                    dve.wait_ge(res_in[u], (n - u) * 8 + 16)
                    dve.wait_ge(y_out[u], (n - u) * 8)
                nc.vector.tensor_tensor(
                    y[:, u, :].rearrange("p (r w) -> p r w", r=BR),
                    res[:, u, :].rearrange("p (r w) -> p r w", r=BR),
                    bank[B_CONV].rearrange("p (w r) -> p r w", r=BR), ALU.add).then_inc(y_ready, 1)

            def prologue():
                dve.wait_ge(in_off, 64)
                split_offsets(0, 0, 0)
                for k in range(TAPS):
                    taps(0, 0, k)
                for g in range(TGROUPS):
                    copy_windows(0, 0, g)
                split_offsets(1, 1, 0)

            bands(dve, {"c": add_x1, "k": taps, "T": copy_windows, "O": split_offsets}, prologue)

            dve.wait_ge(off_chain, OFF_CHAIN * BANDS)
            after_wait(dve)
            dve.sem_inc(far_step, 1)
            dve.wait_ge(far_step, 2)
            nc.vector.tensor_reduce(far_band[:], bank[B_OFF][0:BANDS, 0:NOFF], AX.X,
                                    ALU.max).then_inc(far_step, 1)
            dve.wait_ge(far_step, 4)
            nc.vector.tensor_reduce(far_any[:], bank[B_OFF][0:1, 0:BANDS], AX.X,
                                    ALU.max).then_inc(far_step, 1)
            nc.vector.tensor_scalar(flags[:], bank[B_OFF][0:1, 0:BANDS], float(REACH * REACH),
                                    None, ALU.is_gt).then_inc(flags_ready, 1)
            dve.wait_ge(far_step, 5)
            nc.vector.tensor_scalar(any_flag[:], far_any[:], float(REACH * REACH), None,
                                    ALU.is_gt).then_inc(flags_ready, 1)

            def free_row():
                dve.sem_inc(g_row_ready, 1)

            def first_row():
                nc.vector.memset(band_row[:], -1.0 - BR).then_inc(band_row_set, 1)

            def next_row(img, n):
                dve.wait_ge(band_row_set, img + n + 1)
                nc.vector.tensor_scalar(band_row[:], band_row[:], float(BR), None,
                                        ALU.add).then_inc(band_row_set, 1)
                dve.wait_ge(band_row_set, img + n + 2)
                after_wait(dve)

            def far_band_weights(img, b, n):
                steps = n * (BAND_STEPS + HH * ROW_STEPS)

                def step(ins, j, base=None):
                    ins.then_inc(g_step, 1)
                    dve.wait_ge(g_step, (steps if base is None else base) + j)

                dve.wait_ge(g_raw_in, 16 * n + 16)
                step(nc.vector.tensor_copy(
                    norm_now[:], norm_band[:].rearrange("p j b n -> p j (b n)")
                    [:, :, bass.ds(n, 1)].rearrange("p j n -> p (j n)")), 1)
                step(nc.vector.tensor_scalar(raw[:, 0, :], raw[:, 0, :], norm_now[:, 0:1],
                                             norm_now[:, 1:2], ALU.mult, ALU.add), 2)
                nc.vector.tensor_scalar(
                    z[:, 0], raw[:, 0, :].rearrange("p (r w) -> p w r", r=SRC_R), 0.0, None,
                    ALU.max).then_inc(g_z_ready, 1)
                dve.wait_ge(g_off_done, n + 1)
                step(nc.vector.tensor_scalar(offs[:], bank[B_OFF][0:NOFF, :], bias_off[:], None,
                                             ALU.add), 3)
                for j in (1, 2, 3):
                    step(nc.vector.tensor_tensor(
                        offs[:], bank[B_OFF][32 * j:32 * j + NOFF, :], offs[:], ALU.add), 3 + j)
                step(nc.vector.tensor_copy(coords[PART0:PART0 + NOFF, :], offs[:]), 7)
                step(nc.vector.tensor_tensor(rest[:], offs[:], coords[PART0:PART0 + NOFF, :],
                                             ALU.subtract), 8)
                step(nc.vector.tensor_copy(middle[:], rest[:]), 9)
                step(nc.vector.tensor_tensor(coords[PART2:PART2 + NOFF, :], rest[:], middle[:],
                                             ALU.subtract), 10)
                nc.vector.tensor_copy(coords[PART1:PART1 + NOFF, :],
                                      middle[:]).then_inc(g_coords_ready, 1)
                step(nc.vector.memset(samples[:], 0.0), 11)
                step(nc.vector.tensor_copy(row_shift[:], band_row[:]), 12)
                after_wait(dve)

                with dve.Fori(0, HH) as h:
                    row = n * HH + h
                    at = (n * (BAND_STEPS + HH * ROW_STEPS) + BAND_STEPS) + h * ROW_STEPS
                    dve.wait_ge(g_row_in, row * 16 + 16)
                    step(nc.vector.tensor_scalar(row_z[:], row_in[:], norm_now[:, 0:1],
                                                 norm_now[:, 1:2], ALU.mult, ALU.add), 1, at)
                    nc.vector.tensor_scalar(row_z[:], row_z[:], 0.0, None,
                                            ALU.max).then_inc(g_row_ready, 1)
                    dve.wait_ge(g_row_turned, row + 1)
                    nc.vector.tensor_copy(row_zT[:], bank[B_CONV][:, 0:P]).then_inc(g_zT_ready, 1)
                    for k in range(TAPS):
                        j = 1 + 4 * k
                        dve.wait_ge(g_coord_done, row * TAPS + k + 1)
                        step(nc.vector.tensor_scalar(far_dist[:, 0, :], pairs[0][:, 0, :],
                                                     row_shift[:], None, ALU.add), j + 1, at)
                        step(nc.vector.tensor_copy(far_dist[:, 1, :], pairs[0][:, 1, :]),
                             j + 2, at)
                        step(nc.vector.scalar_tensor_tensor(
                            out=far_hats[:], in0=far_dist[:], scalar=-1.0, in1=far_dist[:],
                            op0=ALU.mult, op1=ALU.max), j + 3, at)
                        step(nc.vector.tensor_scalar(far_hats[:], far_hats[:], -1.0, 0.0,
                                                     ALU.add, ALU.min), j + 4, at)
                        nc.vector.tensor_tensor(far_weights[:], far_hats[:, 0, :],
                                                far_hats[:, 1, :],
                                                ALU.mult).then_inc(g_weights_ready, 1)
                        dve.wait_ge(g_sampled, row * TAPS + k + 1)
                        nc.vector.tensor_tensor(samples[:, k, :], bank[B_S[0]],
                                                samples[:, k, :], ALU.add).then_inc(g_added, 1)
                    step(nc.vector.tensor_scalar(row_shift[:], row_shift[:], -1.0, None,
                                                 ALU.add), ROW_STEPS, at)

                dve.wait_ge(g_conv_done, n + 1)
                dve.wait_ge(g_res_in, 16 * n + 16)
                nc.vector.tensor_tensor(
                    y[:, 0, :].rearrange("p (r w) -> p r w", r=BR),
                    res[:, 0, :].rearrange("p (r w) -> p r w", r=BR),
                    bank[B_CONV].rearrange("p (w r) -> p r w", r=BR),
                    ALU.add).then_inc(g_y_ready, 1)
                dve.wait_ge(g_y_out, 16 * n + 16)
                after_wait(dve)

            general(dve, far_band_weights,
                    ((g_z_ready, 1), (g_coords_ready, 1), (g_row_ready, HH), (g_zT_ready, HH),
                     (g_weights_ready, HH * TAPS), (g_added, HH * TAPS), (g_y_ready, 1),
                     (g_step, BAND_STEPS + HH * ROW_STEPS)),
                    free_row, first_row, next_row)

        @block.gpsimd
        def _(pool):
            pool.wait_ge(const_set, 6)
            pool.wait_ge(rows_copied, 1)

            def inverse_root(g, s):
                pool.wait_ge(vare_ready, g + 1)
                nc.gpsimd.tensor_tensor(rstd[:, s:s + 1], vare[:, s:s + 1],
                                        minus_half[:, 0:1], ALU.pow).then_inc(rstd_ready, 1)

            inverse_root(0, 0)
            inverse_root(1, 1)

            def group(g, s):
                if isinstance(g, int):
                    pool.wait_ge(x_in[s], 16 * (g // XR + 1))
                else:
                    pool.wait_ge(x_in[s], (g - s) * (16 // XR) + 16)
                wait(pool, x1_ready, g - 1)
                nc.gpsimd.tensor_tensor(
                    x_bo[:, s % 2, :].rearrange("p (f w) -> p f w", f=GC),
                    xg[:, s, :].rearrange("p (f w) -> p f w", f=GC),
                    all_o[:].rearrange("p (f l) -> p f l", f=1).broadcast_to([P, GC, P]),
                    ALU.add).then_inc(xbo_ready, 1)
                if not isinstance(g, int) or g + 2 < GROUPS:
                    inverse_root(g + 2, (s + 2) % XR)

            over(pool, 2, 2, GROUPS, XR, group)

            pool.wait_ge(final, 6)
            nc.gpsimd.tensor_tensor(rstd2[:], vare2[:], minus_half[:],
                                    ALU.pow).then_inc(final, 1)


def kernel(x, L0_conv_Wa, L0_conv_ba, L0_conv_Wb, L0_conv_bb, L0_conv_Wg, L0_conv_bg, L0_conv_Wo,
           L0_conv_bo, L1_conv_w_off, L1_conv_b_off, L1_conv_w_def):
    import ml_dtypes
    import numpy as np
    import concourse.bacc as bacc
    from concourse.bass_utils import run_bass_kernel_spmd

    chan = np.arange(CH)
    group_mask = (chan[:, None] // GC == np.arange(GPI)[None]).astype(np.float32)
    select = np.zeros((P, NOFF, WPIX), np.float32)
    select_all = np.zeros((P, NOFF, P), np.float32)
    q = np.arange(WPIX)
    for k in range(TAPS):
        for d in range(2):
            j = 2 * k + d
            for part in (PART0, PART1, PART2):
                select[part + j, j] = 1
                select_all[part + j, j] = 1
            shift = (k // 3, k % 3)[d]
            own = (q % SRC_R, q // SRC_R)[d]
            select[CONE, j] = REACH + shift - own
            select[CONE + 1 + d, j] = 1
            select_all[CONE, j] = (0, -1)[d] + shift - (0, 1)[d] * np.arange(P)
            select_all[CONE + (1, 3)[d], j] = 1
    w, r = np.divmod(np.arange(BW), BR)
    coords = np.stack([np.ones(BW), r, w % WC, w]).astype(ml_dtypes.bfloat16)

    arrays = {
        "x": x, "Wa": L0_conv_Wa, "ba": L0_conv_ba, "Wb": L0_conv_Wb, "bb": L0_conv_bb,
        "Wg": L0_conv_Wg, "bg": L0_conv_bg, "Wo": L0_conv_Wo, "bo": L0_conv_bo,
        "w_off": np.asarray(L1_conv_w_off).reshape(NOFF, CH, TAPS).transpose(1, 2, 0),
        "b_off": L1_conv_b_off,
        "w_def": np.asarray(L1_conv_w_def).reshape(P, CH, TAPS).transpose(1, 2, 0),
        "ident": np.eye(P, dtype=np.float32), "group_mask": group_mask,
        "select": select.astype(ml_dtypes.bfloat16),
        "select_all": select_all.astype(ml_dtypes.bfloat16), "coords": coords,
    }
    arrays = {f"in_{n}": np.ascontiguousarray(a) for n, a in arrays.items()}
    nc = bacc.Bacc("TRN2", target_bir_lowering=False, num_devices=1)
    args = [nc.dram_tensor(n, a.shape, mybir.dt.from_np(a.dtype), kind="ExternalInput").ap()
            for n, a in arrays.items()]
    out = nc.dram_tensor("out", (IMGS, CH, HH, WW), F32, kind="ExternalOutput").ap()
    preact_conv_kernel(nc, *args, out)
    return run_bass_kernel_spmd(nc, [arrays], core_ids=[0]).results[0]["out"]
```

```python
from contextlib import ExitStack

import concourse.bass as bass
from concourse import mybir

IMGS, CH, HH, WW = 2, 128, 128, 128
P = 128
GC = 4
GROUPS = IMGS * CH // GC
GPI = CH // GC
FG = GC * WW
TAPS, NOFF = 9, 18

REACH = 2
MARGIN = REACH + 1
BR, WC = 4, 6
BPI = HH // BR
BANDS = IMGS * BPI
WINDOWS = -(-WW // WC)
LASTC = WW - (WINDOWS - 1) * WC
SRC_R, SRC_C = BR + 2 * MARGIN, WC + 2 * MARGIN
WPIX = SRC_R * SRC_C
PADR = HH + 2 * MARGIN
PADC = (WINDOWS - 1) * WC + SRC_C
BW = BR * WW
PAIRS = WINDOWS // 2
TGROUPS = -(-WINDOWS // 4)
BELOW_ALL = -1e30
EPS = 1e-5
TINY = 1e-30

ALU = mybir.AluOpType
ACT = mybir.ActivationFunctionType
AX = mybir.AxisListType
F32 = mybir.dt.float32
BF16 = mybir.dt.bfloat16
F16 = mybir.dt.float16
I32 = mybir.dt.int32

PART0, PART1, PART2, CONE = 0, 32, 64, 96
CROWS = 4
AXIS_ROWS = 32
OWN = 3 * TAPS
USED_ROWS = OWN + 2
OFF_CHAIN = 8
BAND_STEPS, ROW_STEPS = 12, 2 + 4 * TAPS
W_STEPS = 11
FINAL_STEPS = 14
KROWS = CONE + CROWS

SAMPLE_SCALE, WEIGHT_TOP = 128.0, 8192.0


def wait(eng, sem, n):
    if isinstance(n, int) and n <= 0:
        return
    eng.wait_ge(sem, n)


def over(eng, first, last, end, step, body):
    for n in range(first):
        body(n, n % step)
    count = (end - first - last) // step * step
    with eng.Fori(0, count // step) as i:
        for u in range(step):
            body(i * step + (first + u), (first + u) % step)
    for n in range(first + count, end):
        body(n, n % step)


def preact_conv_kernel(nc, x, Wa, ba, Wb, bb, Wg, bg, Wo, bo, w_off, b_off, w_def,
                       ident_d, group_mask_d, select_d, select_all_d, coords_d, out):
    with ExitStack() as ctx:
        def sb(name, shape, dt=F32):
            return ctx.enter_context(nc.sbuf_tensor(name, shape, dt))

        def sem(name):
            return ctx.enter_context(nc.semaphore(name))

        x1_pad = nc.dram_tensor("x1_pad", [IMGS, CH, PADR, PADC], F32, kind="Internal").ap()

        pairs = [ctx.enter_context(nc.psum_tensor(f"pair{i}", [P, 2, 512], F32)) for i in range(2)]
        bank = [pairs[0][:, 0], pairs[0][:, 1], pairs[1][:, 0], pairs[1][:, 1]]
        bank += [ctx.enter_context(nc.psum_tensor(f"bank{i}", [P, 512], F32))[:]
                 for i in range(4, 8)]

        ident = sb("ident", [P, P])
        group_mask = sb("group_mask", [P, GPI])
        average = sb("average", [P, P])
        ones_row = sb("ones_row", [1, P])
        minus_half = sb("minus_half", [P, GROUPS])
        minus_one = sb("minus_one", [P, 1])
        w_a, w_b, w_g, w_o = (sb(n, [P, P]) for n in ("w_a", "w_b", "w_g", "w_o"))
        bias_a, bias_g = sb("bias_a", [P, 1]), sb("bias_g", [P, 1])
        row_b, row_o = sb("row_b", [1, P]), sb("row_o", [1, P])
        all_b, all_o = sb("all_b", [P, P]), sb("all_o", [P, P])
        w_offs = sb("w_offs", [P, TAPS, NOFF])
        bias_off = sb("bias_off", [NOFF, 1])
        w_defs = sb("w_defs", [P, TAPS, P])
        w_hi, w_lo = (sb(n, [P, TAPS, P], F16) for n in ("w_hi", "w_lo"))
        w_most = sb("w_most", [P, 1])
        w_top = sb("w_top", [1, 1])
        w_top_all = sb("w_top_all", [P, 1])
        w_scale = sb("w_scale", [P, 1])
        unscale = sb("unscale", [P, 1])
        select = sb("select", [2 * AXIS_ROWS, TAPS, WPIX], BF16)

        XR = 4
        xg = sb("xg", [P, XR, FG])
        st6 = sb("st6", [P, XR, 6])
        mv = sb("mv", [P, XR, 2])
        mg = sb("mg", [P, XR, 2])
        dev = sb("dev", [P, XR])
        dev2 = sb("dev2", [P, XR])
        vare = sb("vare", [P, XR])
        rstd = sb("rstd", [P, XR])
        nbias = sb("nbias", [P, XR])
        xT = sb("xT", [P, FG])
        aT = sb("aT", [P, FG])
        gT = sb("gT", [P, FG])
        bm = sb("bm", [P, FG])
        gated = sb("gated", [P, FG])
        x_bo = sb("x_bo", [P, 2, FG])
        x1g = sb("x1g", [P, XR, GC, PADC])
        pad_rows = sb("pad_rows", [P, MARGIN * PADC])

        s6 = sb("s6", [P, 2, 6])
        mv1 = sb("mv1", [P, 2, 2])
        mv2 = sb("mv2", [P, GROUPS, 2])
        mg2 = sb("mg2", [P, GROUPS, 2])
        devs = sb("devs", [P, GROUPS])
        devs2 = sb("devs2", [P, GROUPS])
        vare2 = sb("vare2", [P, GROUPS])
        rstd2 = sb("rstd2", [P, GROUPS])
        nbias2 = sb("nbias2", [P, GROUPS])
        picked = sb("picked", [P, 2, IMGS, GPI])
        norm_c = sb("norm_c", [P, 2, IMGS])
        norm_band = sb("norm_band", [P, 2, IMGS, BPI])

        w_abs = xg[:].rearrange("p s c -> p (s c)")[:, 0:TAPS * P]
        raw = sb("raw", [P, 2, SRC_R * PADC])
        z = sb("z", [P, 2, PADC, SRC_R])
        offs = sb("offs", [NOFF, BW])
        squares = sb("squares", [NOFF, BW])
        rest = sb("rest", [NOFF, BW])
        middle = sb("middle", [NOFF, BW], BF16)
        parts = sb("parts", [P, BW], BF16)
        coords = sb("coords", [2 * AXIS_ROWS, 2, BW], BF16)
        farthest = sb("farthest", [NOFF, BANDS])
        dist = sb("dist", [P, 2, 2, BW])
        hats = sb("hats", [P, 2, 2, BW])
        weights = sb("weights", [P, 2, TAPS, BW])
        zT = sb("zT", [WPIX, 2, WINDOWS, P])
        samples_hi, samples_lo = (sb(n, [P, 2, TAPS, BW], F16)
                                  for n in ("samples_hi", "samples_lo"))
        res = x_bo
        y = sb("y", [P, 2, BW])

        select_all = sb("select_all", [P, NOFF, P], BF16)
        far_band = sb("far_band", [BANDS, 1])
        far_any = sb("far_any", [1, 1])
        flags = sb("flags", [1, BANDS], I32)
        any_flag = sb("any_flag", [1, 1], I32)
        norm_now = sb("norm_now", [P, 2])
        band_row = sb("band_row", [P, 1])
        row_shift = sb("row_shift", [P, 1])
        row_in = sb("row_in", [P, WW])
        row_z = sb("row_z", [P, WW])
        row_zT = sb("row_zT", [P, P])
        far_dist, far_hats, far_weights = dist[:, 0], hats[:, 0], weights[:, 1, 0]
        samples = weights[:, 0]

        in_f32 = sem("in_f32")
        in_off = sem("in_off")
        in_def = sem("in_def")
        const_set = sem("const_set")
        rows_spread = sem("rows_spread")
        rows_copied = sem("rows_copied")
        x_in = [sem(f"x_in{s}") for s in range(XR)]
        x1_out = [sem(f"x1_out{s}") for s in range(XR)]
        pad_set = sem("pad_set")
        pad_out = sem("pad_out")
        bn_done = sem("bn_done")
        mv_ready = sem("mv_ready")
        mean_summed = sem("mean_summed")
        mg_ready = sem("mg_ready")
        dev_ready = sem("dev_ready")
        dev2_ready = sem("dev2_ready")
        var_summed = sem("var_summed")
        vare_ready = sem("vare_ready")
        rstd_ready = sem("rstd_ready")
        nb_ready = sem("nb_ready")
        x_turned = sem("x_turned")
        xT_ready = sem("xT_ready")
        a_done = sem("a_done")
        b_done = sem("b_done")
        g_done = sem("g_done")
        aT_ready = sem("aT_ready")
        bm_ready = sem("bm_ready")
        gT_ready = sem("gT_ready")
        ab_done = sem("ab_done")
        gated_ready = sem("gated_ready")
        o_done = sem("o_done")
        xbo_ready = sem("xbo_ready")
        x1_ready = sem("x1_ready")
        bn2_done = sem("bn2_done")
        mv1_ready = sem("mv1_ready")
        mv2_ready = sem("mv2_ready")
        final = sem("final")

        raw_in = [sem(f"raw_in{s}") for s in range(2)]
        res_in = [sem(f"res_in{s}") for s in range(2)]
        z_ready = sem("z_ready")
        off_done = sem("off_done")
        off_biased = sem("off_biased")
        off_chain = sem("off_chain")
        parts_ready = sem("parts_ready")
        coords_in = [sem(f"coords_in{s}") for s in range(2)]
        coord_done = sem("coord_done")
        dist_ready = sem("dist_ready")
        hats_ready = sem("hats_ready")
        weights_ready = sem("weights_ready")
        z_turned = sem("z_turned")
        zT_a = sem("zT_a")
        zT_v = sem("zT_v")
        sampled = sem("sampled")
        samples_ready = sem("samples_ready")
        lows_ready = sem("lows_ready")
        squared = sem("squared")
        scaling = sem("scaling")
        conv_done = sem("conv_done")
        y_ready = sem("y_ready")
        y_out = [sem(f"y_out{s}") for s in range(2)]

        far_step = sem("far_step")
        flags_ready = sem("flags_ready")
        waits_taken = sem("waits_taken")
        band_row_set = sem("band_row_set")
        g_raw_in, g_row_in, g_res_in, g_y_out = (sem(f"g_{n}") for n in ("raw_in", "row_in",
                                                                         "res_in", "y_out"))
        g_off_done, g_row_turned, g_coord_done, g_sampled, g_conv_done = (
            sem(f"g_{n}") for n in ("off_done", "row_turned", "coord_done", "sampled", "conv_done"))
        g_step, g_z_ready, g_coords_ready, g_row_ready, g_zT_ready = (
            sem(f"g_{n}") for n in ("step", "z_ready", "coords_ready", "row_ready", "zT_ready"))
        g_weights_ready, g_added, g_y_ready = (
            sem(f"g_{n}") for n in ("weights_ready", "added", "y_ready"))

        def after_wait(eng):
            eng.sem_inc(waits_taken, 1)

        def general(eng, band, per_band, at_start=None, before_image=None, before_band=None):
            eng.wait_ge(flags_ready, 2)
            needed = eng.value_load(any_flag[:], min_val=0, max_val=1)
            with eng.If(needed != 0):
                if at_start:
                    at_start()
                with eng.Fori(0, IMGS) as img:
                    if before_image:
                        before_image()
                    with eng.Fori(0, BPI) as b:
                        n = img * BPI + b
                        if before_band:
                            before_band(img, n)
                        flag = eng.value_load(flags[0:1, bass.ds(n, 1)], min_val=0, max_val=1)
                        with eng.If(flag != 0):
                            band(img, b, n)
                        with eng.Else():
                            for semaphore, count in per_band:
                                eng.sem_inc(semaphore, count)

        x_groups = x.rearrange("b (g f) h w -> (b g) h f w", f=GC)
        x1_groups = x1_pad.rearrange("b (g f) r w -> (b g) r f w", f=GC)
        out_v = out.rearrange("b c h w -> b c (h w)")

        B_T, B_A, B_B, B_G, B_AB, B_O, B_ST = range(7)
        B_ZT, B_S = (4, 5), (6, 7)
        B_OFF, B_CONV = B_ZT

        def zT_copied(n, g):
            a = sum(1 for h in range(g + 1) if h % 2 == 0)
            v = g + 1 - a
            na = (TGROUPS + 1) // 2
            return n * na + a, n * (TGROUPS - na) + v

        def sampled_pair(b):
            return bank[B_S[b]][:, 0:TAPS * 2 * WC * BR].rearrange("p (k c) -> p k c", k=TAPS)

        ORDER = [(step[0], int(step[1:])) for step in (
            "z0 k0 k1 s0 s1 O0 c0 s2 c1 k2 k3 c2 c3 P0 k4 c4 s3 k5 c5 c6 s4 k6 c7 c8 s5 k7 "
            "s6 T0 T1 k8 s7 s8 T2 T3 s9 T4 T5 s10 R0").split()]

        def spread_count(n, u):
            return 96 * (n // 2 + 1) if isinstance(n, int) else (n - u) * 48 + 96

        def bands(eng, stages, prologue):
            prologue()

            def band(n, u):
                for kind, j in ORDER:
                    ahead = {"c": -1, "k": 1, "s": 0, "T": 1, "z": 2, "O": 2, "P": 2,
                             "R": 2}[kind]
                    if isinstance(n, int) and not 0 <= n + ahead < BANDS:
                        continue
                    if kind in stages:
                        stages[kind](n + ahead, (u + ahead) % 2, j)

            over(eng, 3, 4, BANDS + 1, 2, band)

        block = ctx.enter_context(nc.Block())

        @block.sync
        def _(sp):
            def load_x(g, s):
                wait(sp, x_turned, g - XR + 1)
                wait(sp, xbo_ready, g - XR + 1)
                sp.dma_start(xg[:, s, :].rearrange("p (f w) -> p f w", f=GC),
                             x_groups[bass.ds(g, 1)].rearrange("g h f w -> (g h) f w")
                             ).then_inc(x_in[s], 16)

            for g in range(2):
                load_x(g, g)
            for dst, src in ((w_a[:], Wa), (w_b[:], Wb), (w_g[:], Wg), (w_o[:], Wo),
                             (bias_a[:], ba.rearrange("(p a) -> p a", a=1)),
                             (bias_g[:], bg.rearrange("(p a) -> p a", a=1)),
                             (row_b[:], bb.rearrange("(a p) -> a p", a=1)),
                             (row_o[:], bo.rearrange("(a p) -> a p", a=1)),
                             (ident[:], ident_d), (group_mask[:], group_mask_d)):
                sp.dma_start(dst, src).then_inc(in_f32, 16)
            for g in range(2, XR):
                load_x(g, g)
            for dst, src in ((w_offs[:], w_off), (bias_off[:], b_off.rearrange("(p a) -> p a", a=1)),
                             (select[:], select_d)):
                sp.dma_start(dst, src).then_inc(in_off, 16)
            for s in range(2):
                for axis in range(2):
                    at = axis * AXIS_ROWS + OWN
                    sp.dma_start(coords[at:at + 2, s, :],
                                 coords_d[0:2 + axis:1 + axis, :]).then_inc(in_off, 16)
            sp.wait_ge(const_set, 7)
            sp.dma_start(parts[CONE:KROWS, :], coords_d).then_inc(in_off, 16)
            sp.dma_start(w_defs[:], w_def).then_inc(in_def, 16)
            sp.dma_start(select_all[:], select_all_d).then_inc(in_def, 16)
            sp.wait_ge(pad_set, 1)
            for b in range(IMGS):
                for r in (0, PADR - MARGIN):
                    sp.dma_start(x1_pad[b, :, r:r + MARGIN, :].rearrange("c r w -> c (r w)"),
                                 pad_rows[:]).then_inc(pad_out, 16)

            def store_x1(g, s):
                wait(sp, x1_ready, g + 1)
                sp.dma_start(x1_groups[bass.ds(g, 1), MARGIN:MARGIN + HH]
                             .rearrange("g r f w -> (g r) f w"),
                             x1g[:, s]).then_inc(x1_out[s], 16)

            def group(g, s):
                if not isinstance(g, int) or g + XR < GROUPS:
                    load_x(g + XR, s)
                if not isinstance(g, int) or g > 0:
                    store_x1(g - 1, (s - 1) % XR)

            over(sp, 1, XR, GROUPS, XR, group)
            store_x1(GROUPS - 1, (GROUPS - 1) % XR)

            for s in range(XR):
                sp.wait_ge(x1_out[s], 16 * GROUPS // XR)
            sp.wait_ge(pad_out, 16 * 2 * IMGS)

            def load_raw(n, s):
                wait(sp, z_ready, n - 1)
                sp.dma_start(raw[:, s, :],
                             x1_pad[bass.ds(n // BPI, 1), :, bass.ds(n % BPI * BR, SRC_R), :]
                             .rearrange("b c r w -> (b c) (r w)")).then_inc(raw_in[s], 16)

            def load_res(n, s):
                wait(sp, y_ready, n - 1)
                sp.dma_start(res[:, s, :].rearrange("p (r w) -> p r w", r=BR),
                             x1_pad[bass.ds(n // BPI, 1), :, bass.ds(n % BPI * BR + MARGIN, BR),
                                    MARGIN:MARGIN + WW]
                             .rearrange("b c r w -> (b c) r w")).then_inc(res_in[s], 16)

            def store_y(n, s):
                wait(sp, y_ready, n + 1)
                sp.dma_start(out_v[bass.ds(n // BPI, 1), :, bass.ds(n % BPI * BW, BW)]
                             .rearrange("b c q -> (b c) q"), y[:, s, :]).then_inc(y_out[s], 16)

            def spread_parts(n, s):
                wait(sp, parts_ready, n + 1)
                for axis in range(2):
                    for p, part in enumerate((PART0, PART1, PART2)):
                        at = axis * AXIS_ROWS + p * TAPS
                        sp.dma_start(coords[at:at + TAPS, s, :],
                                     parts[part + axis:part + NOFF:2, :]).then_inc(coords_in[s], 16)

            load_raw(0, 0)
            load_raw(1, 1)
            spread_parts(0, 0)
            load_raw(2, 0)

            def band(n, s):
                known = isinstance(n, int)
                if not known or n + 3 < BANDS:
                    load_raw(n + 3, (s + 1) % 2)
                if not known or n + 1 < BANDS:
                    spread_parts(n + 1, (s + 1) % 2)
                if not known or n >= 2:
                    store_y(n - 2, s)
                if not known or n < BANDS:
                    load_res(n, s)

            over(sp, 2, 6, BANDS + 2, 2, band)
            for s in range(2):
                sp.wait_ge(y_out[s], 16 * BANDS // 2)

            def far_band_io(img, b, n):
                sp.dma_start(raw[:, 0, :], x1_pad[bass.ds(img, 1), :, bass.ds(b * BR, SRC_R), :]
                             .rearrange("b c r w -> (b c) (r w)")).then_inc(g_raw_in, 16)
                sp.dma_start(res[:, 0, :].rearrange("p (r w) -> p r w", r=BR),
                             x1_pad[bass.ds(img, 1), :, bass.ds(b * BR + MARGIN, BR),
                                    MARGIN:MARGIN + WW]
                             .rearrange("b c r w -> (b c) r w")).then_inc(g_res_in, 16)
                with sp.Fori(0, HH) as h:
                    sp.wait_ge(g_row_ready, n * HH + h + 1)
                    sp.dma_start(row_in[:], x1_pad[bass.ds(img, 1), :, bass.ds(h + MARGIN, 1),
                                                   MARGIN:MARGIN + WW]
                                 .rearrange("b c r w -> (b c) (r w)")).then_inc(g_row_in, 16)
                sp.wait_ge(g_y_ready, n + 1)
                sp.dma_start(out_v[bass.ds(img, 1), :, bass.ds(b * BW, BW)]
                             .rearrange("b c q -> (b c) q"), y[:, 0, :]).then_inc(g_y_out, 16)
                sp.wait_ge(g_y_out, 16 * n + 16)
                after_wait(sp)

            general(sp, far_band_io, ((g_raw_in, 16), (g_res_in, 16), (g_row_in, 16 * HH),
                                      (g_y_out, 16)))

        @block.tensor
        def _(pe):
            pe.wait_ge(in_f32, 160)
            pe.wait_ge(const_set, 2)
            nc.tensor.matmul(bank[B_B][:, 0:P], ones_row[:], row_b[:], start=True, stop=True)
            nc.tensor.matmul(bank[B_B][:, P:2 * P], ones_row[:], row_o[:], start=True,
                             stop=True).then_inc(rows_spread, 1)

            def mean_sum(g, s):
                wait(pe, mv_ready, g + 1)
                wait(pe, vare_ready, g)
                nc.tensor.matmul(bank[B_ST][:, 0:2], average[:], mv[:, s, :], start=True,
                                 stop=True).then_inc(mean_summed, 1)

            def var_sum(g, s):
                wait(pe, dev2_ready, g + 1)
                nc.tensor.matmul(bank[B_ST][:, 2:3], average[:], dev2[:, s:s + 1], start=True,
                                 stop=True).then_inc(var_summed, 1)

            def turn(g, s):
                wait(pe, xT_ready, g)
                if isinstance(g, int):
                    pe.wait_ge(x_in[s], 16 * (g // XR + 1))
                else:
                    pe.wait_ge(x_in[s], (g - s) * (16 // XR) + 16)
                for f in range(GC):
                    mm = nc.tensor.transpose(bank[B_T][:, f * P:(f + 1) * P],
                                             xg[:, s, f * WW:(f + 1) * WW], ident[:])
                mm.then_inc(x_turned, 1)

            def gate(g):
                wait(pe, gated_ready, g + 1)
                wait(pe, x1_ready, g)
                for f in range(GC):
                    mm = nc.tensor.matmul(bank[B_O][:, f * P:(f + 1) * P],
                                          gated[:, f * P:(f + 1) * P], w_o[:],
                                          start=True, stop=True)
                mm.then_inc(o_done, 1)

            def stats_ahead(g):
                return not isinstance(g, int) or g + 2 < GROUPS

            mean_sum(0, 0)
            var_sum(0, 0)
            mean_sum(1, 1)
            var_sum(1, 1)
            turn(0, 0)

            def group(g, s):
                known = isinstance(g, int)
                pe.wait_ge(xT_ready, g + 1)
                wait(pe, aT_ready, g)
                nc.tensor.matmul(bank[B_A], w_a[:], xT[:], start=True,
                                 stop=True).then_inc(a_done, 1)
                wait(pe, bm_ready, g)
                if known and g == 0:
                    pe.wait_ge(rows_copied, 1)
                for f in range(GC):
                    mm = nc.tensor.matmul(bank[B_B][:, f * P:(f + 1) * P],
                                          xT[:, f * P:(f + 1) * P], w_b[:], start=True, stop=True)
                mm.then_inc(b_done, 1)
                wait(pe, gT_ready, g)
                nc.tensor.matmul(bank[B_G], w_g[:], xT[:], start=True,
                                 stop=True).then_inc(g_done, 1)
                if stats_ahead(g):
                    mean_sum(g + 2, (s + 2) % XR)
                if not known or g > 0:
                    gate(g - 1)
                if stats_ahead(g):
                    var_sum(g + 2, (s + 2) % XR)
                if not known or g + 1 < GROUPS:
                    turn(g + 1, (s + 1) % XR)
                pe.wait_ge(aT_ready, g + 1)
                pe.wait_ge(bm_ready, g + 1)
                wait(pe, gated_ready, g)
                for f in range(GC):
                    mm = nc.tensor.matmul(bank[B_AB][:, f * P:(f + 1) * P],
                                          bm[:, f * P:(f + 1) * P], aT[:, f * P:(f + 1) * P],
                                          start=True, stop=True)
                mm.then_inc(ab_done, 1)

            over(pe, 2, 2, GROUPS, XR, group)
            gate(GROUPS - 1)

            pe.wait_ge(scaling, 2)
            nc.tensor.transpose(bank[B_T][0:1, 0:P], w_most[:], ident[:]).then_inc(scaling, 1)

            pe.wait_ge(mv2_ready, GROUPS)
            nc.tensor.matmul(bank[B_ST][:, 0:2 * GROUPS], average[:],
                             mv2[:].rearrange("p g k -> p (g k)"), start=True,
                             stop=True).then_inc(final, 1)
            pe.wait_ge(final, 4)
            nc.tensor.matmul(bank[B_ST][:, 2 * GROUPS:3 * GROUPS], average[:], devs2[:],
                             start=True, stop=True).then_inc(final, 1)
            pe.wait_ge(scaling, 4)
            nc.tensor.matmul(bank[B_T][:, 0:1], ones_row[:], w_top[:], start=True,
                             stop=True).then_inc(scaling, 1)

            def conv(n, u, k):
                if k == 0:
                    wait(pe, lows_ready, PAIRS * (n + 1))
                    wait(pe, y_ready, n)
                    a, v = zT_copied(n + 1, TGROUPS - 1)
                    if not isinstance(n, int):
                        pe.wait_ge(zT_v, v)
                    elif n + 1 < BANDS:
                        pe.wait_ge(zT_v, v)
                for w_part, part in ((w_hi, samples_hi), (w_lo, samples_hi), (w_hi, samples_lo)):
                    mm = nc.tensor.matmul(bank[B_CONV], w_part[:, k, :], part[:, u, k, :],
                                          start=(k == 0 and (w_part, part) == (w_hi, samples_hi)),
                                          stop=(k == TAPS - 1 and part is samples_lo))
                if k == TAPS - 1:
                    mm.then_inc(conv_done, 1)

            def coordinates(n, u, k):
                b = (TAPS * u + k) % 2
                if k == 0:
                    pe.wait_ge(coords_in[u], spread_count(n, u))
                wait(pe, dist_ready, TAPS * n + k - 1)
                for d in range(2):
                    at = d * AXIS_ROWS
                    mm = nc.tensor.matmul(pairs[b][0:WPIX, d, :],
                                          select[at:at + USED_ROWS, k, :],
                                          coords[at:at + USED_ROWS, u, :], start=True, stop=True,
                                          tile_position=(at, 0))
                mm.then_inc(coord_done, 1)

            def sample(n, u, p):
                b = (PAIRS * u + p) % 2
                if p == 0:
                    wait(pe, weights_ready, TAPS * (n + 1))
                    a, v = zT_copied(n, TGROUPS - 1)
                    pe.wait_ge(zT_a, a)
                    pe.wait_ge(zT_v, v)
                wait(pe, lows_ready, PAIRS * n + p - 1)
                for w in (2 * p, 2 * p + 1):
                    cols = min(WC, WW - w * WC)
                    at = (w % 2) * BR * WC
                    mm = nc.tensor.matmul(
                        sampled_pair(b)[:, :, at:at + BR * cols],
                        zT[:, u, w, :],
                        weights[0:WPIX, u, :, w * WC * BR:(w * WC + cols) * BR],
                        start=True, stop=True)
                mm.then_inc(sampled, 1)

            def turn_windows(n, u, g):
                if g == 0:
                    wait(pe, z_ready, n + 1)
                    m = n + 1 if not isinstance(n, int) or n + 1 < BANDS else n
                    pe.wait_ge(off_biased, m + 1)
                    pe.wait_ge(off_chain, OFF_CHAIN * m + 3)
                elif g == 1:
                    wait(pe, y_ready, n - 1)
                else:
                    a, v = zT_copied(n, g - 2)
                    pe.wait_ge(*((zT_a, a) if g % 2 == 0 else (zT_v, v)))
                ws = range(4 * g, min(4 * g + 4, WINDOWS))
                for w in ws:
                    mm = nc.tensor.transpose(
                        bank[B_ZT[g % 2]][0:WPIX, (w % 4) * P:(w % 4 + 1) * P],
                        z[:, u, w * WC:w * WC + SRC_C, :].rearrange("p w r -> p (w r)"),
                        ident[:])
                mm.then_inc(z_turned, 1)

            def convolve_offsets(u):
                q = 4
                for k in range(TAPS):
                    ky, kx = k // 3, k % 3
                    at = 32 * (k % q)
                    mm = nc.tensor.matmul(
                        bank[B_OFF][at:at + NOFF, :].rearrange("p (w r) -> p w r", r=BR),
                        w_offs[:, k, :],
                        z[:, u, MARGIN - 1 + kx:MARGIN - 1 + kx + WW,
                          MARGIN - 1 + ky:MARGIN - 1 + ky + BR],
                        start=(k < q), stop=(k + q >= TAPS), tile_position=(0, at))
                return mm

            def offsets(n, u, _):
                wait(pe, z_ready, n + 1)
                if not isinstance(n, int) or n > 1:
                    pe.wait_ge(zT_a, zT_copied(n - 2, TGROUPS - 2)[0])
                elif n == 1:
                    pe.wait_ge(off_chain, 3)
                convolve_offsets(u).then_inc(off_done, 1)

            def prologue():
                pe.wait_ge(in_off, 16 * 8)
                offsets(0, 0, 0)
                for k in range(TAPS):
                    coordinates(0, 0, k)
                offsets(1, 1, 0)
                for g in range(TGROUPS):
                    turn_windows(0, 0, g)
                pe.wait_ge(scaling, W_STEPS)
                pe.wait_ge(in_def, 32)

            bands(pe, {"c": conv, "k": coordinates, "s": sample, "T": turn_windows,
                       "O": offsets}, prologue)

            pe.wait_ge(far_step, 1)
            nc.tensor.transpose(bank[B_OFF][0:BANDS, 0:NOFF], farthest[:],
                                ident[0:NOFF, 0:NOFF]).then_inc(far_step, 1)
            pe.wait_ge(far_step, 3)
            nc.tensor.transpose(bank[B_OFF][0:1, 0:BANDS], far_band[:],
                                ident[0:BANDS, 0:BANDS]).then_inc(far_step, 1)

            def far_band_products(img, b, n):
                pe.wait_ge(g_z_ready, n + 1)
                convolve_offsets(0).then_inc(g_off_done, 1)
                pe.wait_ge(g_coords_ready, n + 1)
                after_wait(pe)
                with pe.Fori(0, HH) as h:
                    row = n * HH + h
                    pe.wait_ge(g_row_ready, row + 2)
                    nc.tensor.transpose(bank[B_CONV][:, 0:P], row_z[:],
                                        ident[:]).then_inc(g_row_turned, 1)
                    for k in range(TAPS):
                        for d in range(2):
                            mm = nc.tensor.matmul(pairs[0][:, d, :],
                                                  select_all[0:KROWS, 2 * k + d, :],
                                                  parts[0:KROWS, :], start=True, stop=True)
                        mm.then_inc(g_coord_done, 1)
                        if k == 0:
                            pe.wait_ge(g_zT_ready, row + 1)
                        pe.wait_ge(g_weights_ready, row * TAPS + k + 1)
                        nc.tensor.matmul(bank[B_S[0]], row_zT[:], far_weights, start=True,
                                         stop=True).then_inc(g_sampled, 1)
                pe.wait_ge(g_added, (n + 1) * HH * TAPS)
                for k in range(TAPS):
                    mm = nc.tensor.matmul(bank[B_CONV], w_defs[:, k, :], samples[:, k, :],
                                          start=(k == 0), stop=(k == TAPS - 1))
                mm.then_inc(g_conv_done, 1)
                pe.wait_ge(g_conv_done, n + 1)
                after_wait(pe)

            general(pe, far_band_products,
                    ((g_off_done, 1), (g_row_turned, HH), (g_coord_done, HH * TAPS),
                     (g_sampled, HH * TAPS), (g_conv_done, 1)))

        @block.scalar
        def _(act):
            act.wait_ge(in_f32, 160)

            def norm_x(g, s):
                pe_done = g + 1
                wait(act, x_turned, pe_done)
                wait(act, nb_ready, g + 1)
                wait(act, g_done, g)
                nc.scalar.activation(xT[:], bank[B_T], ACT.Identity,
                                     bias=nbias[:, s:s + 1],
                                     scale=rstd[:, s:s + 1]).then_inc(xT_ready, 1)

            norm_x(0, 0)

            def group(g, s):
                act.wait_ge(a_done, g + 1)
                wait(act, ab_done, g)
                nc.scalar.activation(aT[:], bank[B_A], ACT.Identity,
                                     bias=bias_a[:]).then_inc(aT_ready, 1)
                act.wait_ge(g_done, g + 1)
                wait(act, gated_ready, g)
                nc.scalar.activation(gT[:], bank[B_G], ACT.Sigmoid,
                                     bias=bias_g[:]).then_inc(gT_ready, 1)
                if not isinstance(g, int) or g + 1 < GROUPS:
                    norm_x(g + 1, (s + 1) % XR)

            over(act, 1, 3, GROUPS, XR, group)

            def make_z(n, u, _):
                if isinstance(n, int):
                    act.wait_ge(raw_in[u], 16 * (n // 2 + 1))
                else:
                    act.wait_ge(raw_in[u], (n - u) * 8 + 16)
                wait(act, z_turned, TGROUPS * (n - 1))
                wait(act, off_done, n - 1)
                nc.scalar.activation(
                    z[:, u], raw[:, u, :].rearrange("p (r w) -> p w r", r=SRC_R), ACT.Relu,
                    bias=norm_band[:, 1].rearrange("p b n -> p (b n)")[:, bass.ds(n, 1)],
                    scale=norm_band[:, 0].rearrange("p b n -> p (b n)")[:, bass.ds(n, 1)]
                ).then_inc(z_ready, 1)

            def bias_offsets(n, u, _):
                act.wait_ge(off_done, n + 1)
                wait(act, off_chain, OFF_CHAIN * n)
                nc.scalar.activation(offs[:], bank[B_OFF][0:NOFF, :], ACT.Identity,
                                     bias=bias_off[:]).then_inc(off_biased, 1)

            def distances(n, u, k):
                b = (TAPS * u + k) % 2
                t = TAPS * n + k
                act.wait_ge(coord_done, t + 1)
                wait(act, hats_ready, t - 1)
                nc.scalar.activation(dist[0:WPIX, b], pairs[b][0:WPIX], ACT.Abs).then_inc(dist_ready, 1)

            def copy_samples(n, u, p):
                b = (PAIRS * u + p) % 2
                wait(act, sampled, PAIRS * n + p + 1)
                if p == 0:
                    wait(act, conv_done, n - 1)
                c0, c1 = 2 * p * WC * BR, min(2 * (p + 1) * WC * BR, BW)
                nc.scalar.activation(samples_hi[:, u, :, c0:c1], sampled_pair(b)[:, :, 0:c1 - c0],
                                     ACT.Copy, scale=SAMPLE_SCALE).then_inc(samples_ready, 1)

            def copy_windows(n, u, g):
                if g % 2:
                    return
                wait(act, z_turned, TGROUPS * n + g + 1)
                if g == 0:
                    wait(act, sampled, PAIRS * (n - 1))
                c = min(4, WINDOWS - 4 * g)
                nc.scalar.copy(zT[:, u, 4 * g:4 * g + c, :].rearrange("p w c -> p (w c)"),
                               bank[B_ZT[0]][0:WPIX, 0:c * P]).then_inc(zT_a, 1)

            def prologue():
                act.wait_ge(in_off, 16 * 8)
                act.wait_ge(final, FINAL_STEPS)
                make_z(0, 0, 0)
                make_z(1, 1, 0)
                bias_offsets(0, 0, 0)
                for k in range(TAPS):
                    distances(0, 0, k)
                bias_offsets(1, 1, 0)
                for g in range(TGROUPS):
                    copy_windows(0, 0, g)

            bands(act, {"k": distances, "s": copy_samples, "T": copy_windows, "z": make_z,
                        "O": bias_offsets}, prologue)

        @block.vector
        def _(dve):
            nc.vector.memset(average[:], 1.0 / P).then_inc(const_set, 1)
            nc.vector.memset(ones_row[:], 1.0).then_inc(const_set, 1)
            nc.vector.memset(parts[0:64, :], 0.0).then_inc(const_set, 1)
            nc.vector.memset(parts[64:128, :], 0.0).then_inc(const_set, 1)
            nc.vector.memset(minus_half[:], -0.5).then_inc(const_set, 1)
            nc.vector.memset(minus_one[:], -1.0).then_inc(const_set, 1)
            nc.vector.memset(x1g[:], BELOW_ALL).then_inc(const_set, 1)
            nc.vector.memset(pad_rows[:], BELOW_ALL).then_inc(pad_set, 1)

            dve.wait_ge(rows_spread, 1)
            nc.vector.tensor_copy(all_b[:], bank[B_B][:, 0:P])
            nc.vector.tensor_copy(all_o[:], bank[B_B][:, P:2 * P]).then_inc(rows_copied, 1)
            dve.wait_ge(rows_copied, 1)
            dve.wait_ge(const_set, 7)

            def row_stats(g, s):
                if isinstance(g, int):
                    dve.wait_ge(x_in[s], 16 * (g // XR + 1))
                else:
                    dve.wait_ge(x_in[s], (g - s) * (16 // XR) + 16)
                nc.vector.bn_stats(st6[:, s, :], xg[:, s, :]).then_inc(bn_done, 1)

            def row_means(g, s):
                nc.vector.bn_aggr(mv[:, s, :], st6[:, s, :]).then_inc(mv_ready, 1)

            def deviations(g, s):
                dve.wait_ge(mean_summed, g + 1)
                nc.vector.tensor_copy(mg[:, s, :], bank[B_ST][:, 0:2]).then_inc(mg_ready, 1)
                dve.wait_ge(mg_ready, g + 1)
                nc.vector.tensor_tensor(dev[:, s:s + 1], mv[:, s, 0:1], mg[:, s, 0:1],
                                        ALU.subtract).then_inc(dev_ready, 1)
                dve.wait_ge(dev_ready, g + 1)
                nc.vector.tensor_tensor(dev2[:, s:s + 1], dev[:, s:s + 1], dev[:, s:s + 1],
                                        ALU.mult).then_inc(dev2_ready, 1)

            def variance(g, s):
                dve.wait_ge(var_summed, g + 1)
                nc.vector.scalar_tensor_tensor(
                    out=vare[:, s:s + 1], in0=bank[B_ST][:, 2:3], scalar=EPS,
                    in1=mg[:, s, 1:2], op0=ALU.add, op1=ALU.add).then_inc(vare_ready, 1)

            def norm_bias(g, s):
                dve.wait_ge(rstd_ready, g + 1)
                nc.vector.scalar_tensor_tensor(
                    out=nbias[:, s:s + 1], in0=mg[:, s, 0:1], scalar=-1.0,
                    in1=rstd[:, s:s + 1], op0=ALU.mult, op1=ALU.mult).then_inc(nb_ready, 1)

            def add_x(g, s):
                dve.wait_ge(o_done, g + 1)
                wait(dve, xbo_ready, g + 1)
                if isinstance(g, int):
                    wait(dve, x1_out[s], 16 * (g // XR))
                else:
                    dve.wait_ge(x1_out[s], (g - s) * (16 // XR))
                h = x1g[:, s, :, MARGIN:MARGIN + WW]
                nc.vector.tensor_tensor(
                    h, bank[B_O].rearrange("p (f w) -> p f w", f=GC),
                    x_bo[:, s % 2, :].rearrange("p (f w) -> p f w", f=GC),
                    ALU.add).then_inc(x1_ready, 1)
                dve.wait_ge(x1_ready, g + 1)
                nc.vector.bn_stats(s6[:, s % 2, :], h).then_inc(bn2_done, 1)

            def x1_means(g, s):
                nc.vector.bn_aggr(mv1[:, s % 2, :], s6[:, s % 2, :]).then_inc(mv1_ready, 1)

            def keep_x1_means(g, s):
                dve.wait_ge(mv1_ready, g + 1)
                nc.vector.tensor_copy(mv2[:, bass.ds(g, 1), :].rearrange("p g k -> p (g k)"),
                                      mv1[:, s % 2, :]).then_inc(mv2_ready, 1)

            for g in range(2):
                row_stats(g, g)
                dve.wait_ge(bn_done, g + 1)
                row_means(g, g)
                deviations(g, g)
                variance(g, g)
                norm_bias(g, g)

            def group(g, s):
                known = isinstance(g, int)
                ahead = not known or g + 2 < GROUPS
                t = (s + 2) % XR
                if ahead:
                    row_stats(g + 2, t)
                dve.wait_ge(b_done, g + 1)
                wait(dve, ab_done, g)
                if ahead:
                    dve.wait_ge(bn_done, g + 3)
                nc.vector.tensor_tensor(
                    bm[:].rearrange("p (f l) -> p f l", f=GC),
                    bank[B_B].rearrange("p (f l) -> p f l", f=GC),
                    all_b[:].rearrange("p (f l) -> p f l", f=1).broadcast_to([P, GC, P]),
                    ALU.add).then_inc(bm_ready, 1)
                if ahead:
                    row_means(g + 2, t)
                    deviations(g + 2, t)
                behind = not known or g > 0
                if behind:
                    add_x(g - 1, (s - 1) % XR)
                    dve.wait_ge(bn2_done, g)
                if ahead:
                    variance(g + 2, t)
                if behind:
                    x1_means(g - 1, (s - 1) % XR)
                if ahead:
                    norm_bias(g + 2, t)
                if behind:
                    keep_x1_means(g - 1, (s - 1) % XR)
                dve.wait_ge(ab_done, g + 1)
                dve.wait_ge(gT_ready, g + 1)
                wait(dve, o_done, g)
                nc.vector.tensor_tensor(gated[:], bank[B_AB], gT[:],
                                        ALU.mult).then_inc(gated_ready, 1)

            over(dve, 1 + XR, 3, GROUPS, XR, group)
            last = (GROUPS - 1, (GROUPS - 1) % XR)
            add_x(*last)
            dve.wait_ge(bn2_done, GROUPS)
            x1_means(*last)
            keep_x1_means(*last)

            w_flat = w_defs[:].rearrange("p k c -> p (k c)")
            dve.wait_ge(in_def, 32)
            nc.vector.scalar_tensor_tensor(out=w_abs, in0=w_flat, scalar=-1.0, in1=w_flat,
                                           op0=ALU.mult, op1=ALU.max).then_inc(scaling, 1)
            dve.wait_ge(scaling, 1)
            nc.vector.tensor_reduce(w_most[:], w_abs, AX.X, ALU.max).then_inc(scaling, 1)

            dve.wait_ge(final, 1)
            nc.vector.tensor_copy(mg2[:].rearrange("p g k -> p (g k)"),
                                  bank[B_ST][:, 0:2 * GROUPS]).then_inc(final, 1)
            dve.wait_ge(final, 2)
            nc.vector.tensor_tensor(devs[:], mv2[:, :, 0], mg2[:, :, 0],
                                    ALU.subtract).then_inc(final, 1)
            dve.wait_ge(final, 3)
            nc.vector.tensor_tensor(devs2[:], devs[:], devs[:], ALU.mult).then_inc(final, 1)
            dve.wait_ge(scaling, 3)
            nc.vector.tensor_reduce(w_top[:], bank[B_T][0:1, 0:P], AX.X,
                                    ALU.max).then_inc(scaling, 1)
            dve.wait_ge(final, 5)
            nc.vector.scalar_tensor_tensor(
                out=vare2[:], in0=bank[B_ST][:, 2 * GROUPS:3 * GROUPS], scalar=EPS,
                in1=mg2[:, :, 1], op0=ALU.add, op1=ALU.add).then_inc(final, 1)
            dve.wait_ge(final, 7)
            nc.vector.scalar_tensor_tensor(
                out=nbias2[:], in0=mg2[:, :, 0], scalar=-1.0, in1=rstd2[:],
                op0=ALU.mult, op1=ALU.mult).then_inc(final, 1)
            dve.wait_ge(final, 8)
            for j, per_group in enumerate((rstd2, nbias2)):
                nc.vector.tensor_tensor(
                    picked[:, j], per_group[:].rearrange("p (b g) -> p b g", b=IMGS),
                    group_mask[:].rearrange("p (b g) -> p b g", b=1)
                    .broadcast_to([P, IMGS, GPI]), ALU.mult).then_inc(final, 1)
            dve.wait_ge(final, 10)
            for j in range(2):
                nc.vector.tensor_reduce(norm_c[:, j, :], picked[:, j], AX.X,
                                        ALU.add).then_inc(final, 1)
            dve.wait_ge(final, 12)
            for j in range(2):
                nc.vector.tensor_copy(
                    norm_band[:, j],
                    norm_c[:, j, :].rearrange("p (b n) -> p b n", n=1)
                    .broadcast_to([P, IMGS, BPI])).then_inc(final, 1)
            dve.wait_ge(scaling, 5)
            nc.vector.tensor_scalar(w_top_all[:], bank[B_T][:, 0:1], TINY, None,
                                    ALU.max).then_inc(scaling, 1)

            def make_hats(n, u, k):
                b = (TAPS * u + k) % 2
                t = TAPS * n + k
                dve.wait_ge(dist_ready, t + 1)
                wait(dve, weights_ready, t - 1)
                nc.vector.tensor_scalar(hats[0:WPIX, b], dist[0:WPIX, b], -1.0, 0.0, ALU.add,
                                        ALU.min).then_inc(hats_ready, 1)

            def copy_samples_lo(n, u, p):
                b = (PAIRS * u + p) % 2
                wait(dve, samples_ready, PAIRS * n + p + 1)
                if p == 0:
                    wait(dve, conv_done, n - 1)
                c0, c1 = 2 * p * WC * BR, min(2 * (p + 1) * WC * BR, BW)
                nc.vector.scalar_tensor_tensor(
                    out=samples_lo[:, u, :, c0:c1], in0=sampled_pair(b)[:, :, 0:c1 - c0],
                    scalar=SAMPLE_SCALE, in1=samples_hi[:, u, :, c0:c1],
                    op0=ALU.mult, op1=ALU.subtract).then_inc(lows_ready, 1)

            def sum_offsets(n, u, _):
                for j in range(3):
                    dve.wait_ge(*((off_chain, OFF_CHAIN * n + j) if j else (off_biased, n + 1)))
                    nc.vector.tensor_tensor(
                        offs[:], bank[B_OFF][32 * (j + 1):32 * (j + 1) + NOFF, :], offs[:],
                        ALU.add).then_inc(off_chain, 1)

            def split_offsets(n, u, _):
                c = OFF_CHAIN * n

                def done(ins, j):
                    ins.then_inc(off_chain, 1)
                    dve.wait_ge(off_chain, c + j)

                dve.wait_ge(off_chain, c + 3)
                if not isinstance(n, int) or n > 0:
                    dve.wait_ge(coords_in[1 - u], spread_count(n - 1, 1 - u))
                done(nc.vector.tensor_copy(parts[PART0:PART0 + NOFF, :], offs[:]), 4)
                done(nc.vector.tensor_tensor(rest[:], offs[:], parts[PART0:PART0 + NOFF, :],
                                             ALU.subtract), 5)
                done(nc.vector.tensor_copy(middle[:], rest[:]), 6)
                done(nc.vector.tensor_tensor(parts[PART2:PART2 + NOFF, :], rest[:], middle[:],
                                             ALU.subtract), 7)
                nc.vector.tensor_copy(parts[PART1:PART1 + NOFF, :],
                                      middle[:]).then_inc(parts_ready, 1)

            def reach(n, u, _):
                dve.wait_ge(squared, n + 1)
                nc.vector.tensor_reduce(farthest[:, bass.ds(n, 1)], squares[:], AX.X,
                                        ALU.max).then_inc(off_chain, 1)

            def copy_windows(n, u, g):
                if g % 2 == 0:
                    return
                dve.wait_ge(z_turned, TGROUPS * n + g + 1)
                if g == 1:
                    wait(dve, sampled, PAIRS * (n - 1))
                c = min(4, WINDOWS - 4 * g)
                nc.vector.tensor_copy(zT[:, u, 4 * g:4 * g + c, :].rearrange("p w c -> p (w c)"),
                                      bank[B_ZT[1]][0:WPIX, 0:c * P]).then_inc(zT_v, 1)

            def add_x1(n, u, k):
                if k < TAPS - 1:
                    return
                dve.wait_ge(conv_done, n + 1)
                if isinstance(n, int):
                    dve.wait_ge(res_in[u], 16 * (n // 2 + 1))
                    wait(dve, y_out[u], 16 * (n // 2))
                else:
                    dve.wait_ge(res_in[u], (n - u) * 8 + 16)
                    dve.wait_ge(y_out[u], (n - u) * 8)
                nc.vector.scalar_tensor_tensor(
                    out=y[:, u, :].rearrange("p (r w) -> p r w", r=BR),
                    in0=bank[B_CONV].rearrange("p (w r) -> p r w", r=BR), scalar=unscale[:],
                    in1=res[:, u, :].rearrange("p (r w) -> p r w", r=BR),
                    op0=ALU.mult, op1=ALU.add).then_inc(y_ready, 1)

            def prologue():
                dve.wait_ge(in_off, 16 * 8)
                sum_offsets(0, 0, 0)
                split_offsets(0, 0, 0)
                reach(0, 0, 0)
                for k in range(TAPS):
                    make_hats(0, 0, k)
                sum_offsets(1, 1, 0)
                split_offsets(1, 1, 0)
                reach(1, 1, 0)
                for g in range(TGROUPS):
                    copy_windows(0, 0, g)

            bands(dve, {"c": add_x1, "k": make_hats, "s": copy_samples_lo, "T": copy_windows, "O": sum_offsets,
                        "P": split_offsets, "R": reach}, prologue)

            dve.wait_ge(off_chain, OFF_CHAIN * BANDS)
            after_wait(dve)
            dve.sem_inc(far_step, 1)
            dve.wait_ge(far_step, 2)
            nc.vector.tensor_reduce(far_band[:], bank[B_OFF][0:BANDS, 0:NOFF], AX.X,
                                    ALU.max).then_inc(far_step, 1)
            dve.wait_ge(far_step, 4)
            nc.vector.tensor_reduce(far_any[:], bank[B_OFF][0:1, 0:BANDS], AX.X,
                                    ALU.max).then_inc(far_step, 1)
            nc.vector.tensor_scalar(flags[:], bank[B_OFF][0:1, 0:BANDS], float(REACH * REACH),
                                    None, ALU.is_gt).then_inc(flags_ready, 1)
            dve.wait_ge(far_step, 5)
            nc.vector.tensor_scalar(any_flag[:], far_any[:], float(REACH * REACH), None,
                                    ALU.is_gt).then_inc(flags_ready, 1)

            def free_row():
                dve.sem_inc(g_row_ready, 1)

            def first_row():
                nc.vector.memset(band_row[:], -1.0 - BR).then_inc(band_row_set, 1)

            def next_row(img, n):
                dve.wait_ge(band_row_set, img + n + 1)
                nc.vector.tensor_scalar(band_row[:], band_row[:], float(BR), None,
                                        ALU.add).then_inc(band_row_set, 1)
                dve.wait_ge(band_row_set, img + n + 2)
                after_wait(dve)

            def far_band_weights(img, b, n):
                steps = n * (BAND_STEPS + HH * ROW_STEPS)

                def step(ins, j, base=None):
                    ins.then_inc(g_step, 1)
                    dve.wait_ge(g_step, (steps if base is None else base) + j)

                dve.wait_ge(g_raw_in, 16 * n + 16)
                step(nc.vector.tensor_copy(
                    norm_now[:], norm_band[:].rearrange("p j b n -> p j (b n)")
                    [:, :, bass.ds(n, 1)].rearrange("p j n -> p (j n)")), 1)
                step(nc.vector.tensor_scalar(raw[:, 0, :], raw[:, 0, :], norm_now[:, 0:1],
                                             norm_now[:, 1:2], ALU.mult, ALU.add), 2)
                nc.vector.tensor_scalar(
                    z[:, 0], raw[:, 0, :].rearrange("p (r w) -> p w r", r=SRC_R), 0.0, None,
                    ALU.max).then_inc(g_z_ready, 1)
                dve.wait_ge(g_off_done, n + 1)
                step(nc.vector.tensor_scalar(offs[:], bank[B_OFF][0:NOFF, :], bias_off[:], None,
                                             ALU.add), 3)
                for j in (1, 2, 3):
                    step(nc.vector.tensor_tensor(
                        offs[:], bank[B_OFF][32 * j:32 * j + NOFF, :], offs[:], ALU.add), 3 + j)
                step(nc.vector.tensor_copy(parts[PART0:PART0 + NOFF, :], offs[:]), 7)
                step(nc.vector.tensor_tensor(rest[:], offs[:], parts[PART0:PART0 + NOFF, :],
                                             ALU.subtract), 8)
                step(nc.vector.tensor_copy(middle[:], rest[:]), 9)
                step(nc.vector.tensor_tensor(parts[PART2:PART2 + NOFF, :], rest[:], middle[:],
                                             ALU.subtract), 10)
                nc.vector.tensor_copy(parts[PART1:PART1 + NOFF, :],
                                      middle[:]).then_inc(g_coords_ready, 1)
                step(nc.vector.memset(samples[:], 0.0), 11)
                step(nc.vector.tensor_copy(row_shift[:], band_row[:]), 12)
                after_wait(dve)

                with dve.Fori(0, HH) as h:
                    row = n * HH + h
                    at = (n * (BAND_STEPS + HH * ROW_STEPS) + BAND_STEPS) + h * ROW_STEPS
                    dve.wait_ge(g_row_in, row * 16 + 16)
                    step(nc.vector.tensor_scalar(row_z[:], row_in[:], norm_now[:, 0:1],
                                                 norm_now[:, 1:2], ALU.mult, ALU.add), 1, at)
                    nc.vector.tensor_scalar(row_z[:], row_z[:], 0.0, None,
                                            ALU.max).then_inc(g_row_ready, 1)
                    dve.wait_ge(g_row_turned, row + 1)
                    nc.vector.tensor_copy(row_zT[:], bank[B_CONV][:, 0:P]).then_inc(g_zT_ready, 1)
                    for k in range(TAPS):
                        j = 1 + 4 * k
                        dve.wait_ge(g_coord_done, row * TAPS + k + 1)
                        step(nc.vector.tensor_scalar(far_dist[:, 0, :], pairs[0][:, 0, :],
                                                     row_shift[:], None, ALU.add), j + 1, at)
                        step(nc.vector.tensor_copy(far_dist[:, 1, :], pairs[0][:, 1, :]),
                             j + 2, at)
                        step(nc.vector.scalar_tensor_tensor(
                            out=far_hats, in0=far_dist, scalar=-1.0, in1=far_dist,
                            op0=ALU.mult, op1=ALU.max), j + 3, at)
                        step(nc.vector.tensor_scalar(far_hats, far_hats, -1.0, 0.0,
                                                     ALU.add, ALU.min), j + 4, at)
                        nc.vector.tensor_tensor(far_weights, far_hats[:, 0, :],
                                                far_hats[:, 1, :],
                                                ALU.mult).then_inc(g_weights_ready, 1)
                        dve.wait_ge(g_sampled, row * TAPS + k + 1)
                        nc.vector.tensor_tensor(samples[:, k, :], bank[B_S[0]],
                                                samples[:, k, :], ALU.add).then_inc(g_added, 1)
                    step(nc.vector.tensor_scalar(row_shift[:], row_shift[:], -1.0, None,
                                                 ALU.add), ROW_STEPS, at)

                dve.wait_ge(g_conv_done, n + 1)
                dve.wait_ge(g_res_in, 16 * n + 16)
                nc.vector.tensor_tensor(
                    y[:, 0, :].rearrange("p (r w) -> p r w", r=BR),
                    res[:, 0, :].rearrange("p (r w) -> p r w", r=BR),
                    bank[B_CONV].rearrange("p (w r) -> p r w", r=BR),
                    ALU.add).then_inc(g_y_ready, 1)
                dve.wait_ge(g_y_out, 16 * n + 16)
                after_wait(dve)

            general(dve, far_band_weights,
                    ((g_z_ready, 1), (g_coords_ready, 1), (g_row_ready, HH), (g_zT_ready, HH),
                     (g_weights_ready, HH * TAPS), (g_added, HH * TAPS), (g_y_ready, 1),
                     (g_step, BAND_STEPS + HH * ROW_STEPS)),
                    free_row, first_row, next_row)

        @block.gpsimd
        def _(pool):
            pool.wait_ge(const_set, 7)
            pool.wait_ge(rows_copied, 1)

            def inverse_root(g, s):
                pool.wait_ge(vare_ready, g + 1)
                nc.gpsimd.tensor_tensor(rstd[:, s:s + 1], vare[:, s:s + 1],
                                        minus_half[:, 0:1], ALU.pow).then_inc(rstd_ready, 1)

            inverse_root(0, 0)
            inverse_root(1, 1)

            def group(g, s):
                if isinstance(g, int):
                    pool.wait_ge(x_in[s], 16 * (g // XR + 1))
                else:
                    pool.wait_ge(x_in[s], (g - s) * (16 // XR) + 16)
                wait(pool, x1_ready, g - 1)
                nc.gpsimd.tensor_tensor(
                    x_bo[:, s % 2, :].rearrange("p (f w) -> p f w", f=GC),
                    xg[:, s, :].rearrange("p (f w) -> p f w", f=GC),
                    all_o[:].rearrange("p (f l) -> p f l", f=1).broadcast_to([P, GC, P]),
                    ALU.add).then_inc(xbo_ready, 1)
                if not isinstance(g, int) or g + 2 < GROUPS:
                    inverse_root(g + 2, (s + 2) % XR)

            over(pool, 2, 2, GROUPS, XR, group)

            pool.wait_ge(final, 6)
            nc.gpsimd.tensor_tensor(rstd2[:], vare2[:], minus_half[:],
                                    ALU.pow).then_inc(final, 1)
            pool.wait_ge(scaling, 6)
            nc.gpsimd.tensor_tensor(w_scale[:], w_top_all[:], minus_one[:],
                                    ALU.pow).then_inc(scaling, 1)

            def weigh(n, u, k):
                b = (TAPS * u + k) % 2
                pool.wait_ge(hats_ready, TAPS * n + k + 1)
                if k == 0:
                    wait(pool, sampled, PAIRS * (n - 1))
                nc.gpsimd.tensor_tensor(weights[0:WPIX, u, k, :], hats[0:WPIX, b, 0, :],
                                        hats[0:WPIX, b, 1, :], ALU.mult).then_inc(weights_ready, 1)

            def square_offsets(n, u, _):
                pool.wait_ge(off_chain, OFF_CHAIN * n + 3)
                nc.gpsimd.tensor_tensor(squares[:], offs[:], offs[:],
                                        ALU.mult).then_inc(squared, 1)

            def prologue():
                square_offsets(0, 0, 0)
                for k in range(TAPS):
                    weigh(0, 0, k)
                square_offsets(1, 1, 0)
                pool.wait_ge(scaling, 7)
                nc.gpsimd.tensor_scalar(
                    w_abs, w_defs[:].rearrange("p k c -> p (k c)"), w_scale[:], WEIGHT_TOP,
                    ALU.mult, ALU.mult).then_inc(scaling, 1)
                pool.wait_ge(scaling, 8)
                nc.gpsimd.tensor_copy(w_hi[:].rearrange("p k c -> p (k c)"),
                                      w_abs).then_inc(scaling, 1)
                pool.wait_ge(scaling, 9)
                nc.gpsimd.tensor_tensor(
                    w_lo[:].rearrange("p k c -> p (k c)"), w_abs,
                    w_hi[:].rearrange("p k c -> p (k c)"), ALU.subtract).then_inc(scaling, 1)
                nc.gpsimd.tensor_scalar(unscale[:], w_top_all[:], 1 / (SAMPLE_SCALE * WEIGHT_TOP),
                                        None, ALU.mult).then_inc(scaling, 1)

            bands(pool, {"k": weigh, "P": square_offsets}, prologue)


def kernel(x, L0_conv_Wa, L0_conv_ba, L0_conv_Wb, L0_conv_bb, L0_conv_Wg, L0_conv_bg, L0_conv_Wo,
           L0_conv_bo, L1_conv_w_off, L1_conv_b_off, L1_conv_w_def):
    import ml_dtypes
    import numpy as np
    import concourse.bacc as bacc
    from concourse.bass_utils import run_bass_kernel_spmd

    chan = np.arange(CH)
    group_mask = (chan[:, None] // GC == np.arange(GPI)[None]).astype(np.float32)
    select = np.zeros((2 * AXIS_ROWS, TAPS, WPIX), np.float32)
    select_all = np.zeros((P, NOFF, P), np.float32)
    q = np.arange(WPIX)
    for k in range(TAPS):
        for d in range(2):
            j = 2 * k + d
            for p, part in enumerate((PART0, PART1, PART2)):
                select[d * AXIS_ROWS + p * TAPS + k, k] = 1
                select_all[part + j, j] = 1
            shift = (k // 3, k % 3)[d]
            own = (q % SRC_R, q // SRC_R)[d]
            select[d * AXIS_ROWS + OWN, k] = REACH + shift - own
            select[d * AXIS_ROWS + OWN + 1, k] = 1
            select_all[CONE, j] = (0, -1)[d] + shift - (0, 1)[d] * np.arange(P)
            select_all[CONE + (1, 3)[d], j] = 1
    w, r = np.divmod(np.arange(BW), BR)
    coords = np.stack([np.ones(BW), r, w % WC, w]).astype(ml_dtypes.bfloat16)

    arrays = {
        "x": x, "Wa": L0_conv_Wa, "ba": L0_conv_ba, "Wb": L0_conv_Wb, "bb": L0_conv_bb,
        "Wg": L0_conv_Wg, "bg": L0_conv_bg, "Wo": L0_conv_Wo, "bo": L0_conv_bo,
        "w_off": np.asarray(L1_conv_w_off).reshape(NOFF, CH, TAPS).transpose(1, 2, 0),
        "b_off": L1_conv_b_off,
        "w_def": np.asarray(L1_conv_w_def).reshape(P, CH, TAPS).transpose(1, 2, 0),
        "ident": np.eye(P, dtype=np.float32), "group_mask": group_mask,
        "select": select.astype(ml_dtypes.bfloat16),
        "select_all": select_all.astype(ml_dtypes.bfloat16), "coords": coords,
    }
    arrays = {f"in_{n}": np.ascontiguousarray(a) for n, a in arrays.items()}
    nc = bacc.Bacc("TRN2", target_bir_lowering=False, num_devices=1)
    args = [nc.dram_tensor(n, a.shape, mybir.dt.from_np(a.dtype), kind="ExternalInput").ap()
            for n, a in arrays.items()]
    out = nc.dram_tensor("out", (IMGS, CH, HH, WW), F32, kind="ExternalOutput").ap()
    preact_conv_kernel(nc, *args, out)
    return run_bass_kernel_spmd(nc, [arrays], core_ids=[0]).results[0]["out"]
```

```python
from contextlib import ExitStack

import concourse.bass as bass
from concourse import mybir

IMGS, CH, HH, WW = 2, 128, 128, 128
P = 128
GC = 4
GROUPS = IMGS * CH // GC
GPI = CH // GC
FG = GC * WW
TAPS, NOFF = 9, 18

REACH = 2
MARGIN = REACH + 1
BR, WC = 4, 6
BPI = HH // BR
BANDS = IMGS * BPI
WINDOWS = -(-WW // WC)
LASTC = WW - (WINDOWS - 1) * WC
SRC_R, SRC_C = BR + 2 * MARGIN, WC + 2 * MARGIN
WPIX = SRC_R * SRC_C
PADR = HH + 2 * MARGIN
PADC = (WINDOWS - 1) * WC + SRC_C
BW = BR * WW
PAIRS = WINDOWS // 2
TGROUPS = -(-WINDOWS // 4)
BELOW_ALL = -1e30
EPS = 1e-5
TINY = 1e-30

ALU = mybir.AluOpType
ACT = mybir.ActivationFunctionType
AX = mybir.AxisListType
F32 = mybir.dt.float32
BF16 = mybir.dt.bfloat16
F16 = mybir.dt.float16
I32 = mybir.dt.int32

PART0, PART1, PART2, CONE = 0, 32, 64, 96
CROWS = 4
AXIS_ROWS = 32
OWN = 3 * TAPS
USED_ROWS = OWN + 2
OFF_CHAIN = 8
BAND_STEPS, ROW_STEPS = 12, 2 + 4 * TAPS
ABG_STEPS = 11
W_STEPS = 16
FINAL_STEPS = 14
KROWS = CONE + CROWS

PIXEL_SCALE, WEIGHT_TOP = 128.0, 8192.0
DEF, OFF = 0, 1


def wait(eng, sem, n):
    if isinstance(n, int) and n <= 0:
        return
    eng.wait_ge(sem, n)


def over(eng, first, last, end, step, body):
    for n in range(first):
        body(n, n % step)
    count = (end - first - last) // step * step
    with eng.Fori(0, count // step) as i:
        for u in range(step):
            body(i * step + (first + u), (first + u) % step)
    for n in range(first + count, end):
        body(n, n % step)


def preact_conv_kernel(nc, x, Wa, ba, Wb, bb, Wg, bg, Wo, bo, w_off, b_off, w_def,
                       ident_d, group_mask_d, select_d, select_all_d, coords_d, out):
    with ExitStack() as ctx:
        def sb(name, shape, dt=F32):
            return ctx.enter_context(nc.sbuf_tensor(name, shape, dt))

        def sem(name):
            return ctx.enter_context(nc.semaphore(name))

        x1_pad = nc.dram_tensor("x1_pad", [IMGS, CH, PADR, PADC], F32, kind="Internal").ap()

        pairs = [ctx.enter_context(nc.psum_tensor(f"pair{i}", [P, 2, 512], F32)) for i in range(2)]
        bank = [pairs[0][:, 0], pairs[0][:, 1], pairs[1][:, 0], pairs[1][:, 1]]
        bank += [ctx.enter_context(nc.psum_tensor(f"bank{i}", [P, 512], F32))[:]
                 for i in range(4, 8)]

        XR, BATCH = 8, 4
        ident = sb("ident", [P, P])
        group_mask = sb("group_mask", [P, GPI])
        average = sb("average", [P, P])
        ones_row = sb("ones_row", [1, P])
        minus_half = sb("minus_half", [P, BATCH])
        minus_one = sb("minus_one", [P, 3])
        w_abg, w_abg_work = sb("w_abg", [P, 3, P]), sb("w_abg_work", [P, 3, P])
        w_abg_hi, w_abg_lo = (sb(n, [P, 3, P], F16) for n in ("w_abg_hi", "w_abg_lo"))
        abg_most, abg_top = sb("abg_most", [P, 3]), sb("abg_top", [1, 3])
        abg_top_all, abg_scale, abg_unscale = (
            sb(n, [P, 3]) for n in ("abg_top_all", "abg_scale", "abg_unscale"))
        w_o = sb("w_o", [P, P])
        xT_hi, xT_lo = (sb(n, [P, FG], F16) for n in ("xT_hi", "xT_lo"))
        bias_a, bias_g = sb("bias_a", [P, 1]), sb("bias_g", [P, 1])
        row_b, row_o = sb("row_b", [1, P]), sb("row_o", [1, P])
        all_b, all_o = sb("all_b", [P, P]), sb("all_o", [P, P])
        w_offs = sb("w_offs", [P, TAPS, NOFF])
        bias_off = sb("bias_off", [NOFF, 1])
        w_defs = sb("w_defs", [P, TAPS, P])
        w_hi, w_lo = (sb(n, [P, TAPS, P], F16) for n in ("w_hi", "w_lo"))
        woff_hi, woff_lo = (sb(n, [P, TAPS, NOFF], F16) for n in ("woff_hi", "woff_lo"))
        w_most = sb("w_most", [P, 2])
        w_top = sb("w_top", [1, 2])
        w_top_all, w_scale, unscale = (sb(n, [P, 2]) for n in ("w_top_all", "w_scale", "unscale"))
        select = sb("select", [2 * AXIS_ROWS, TAPS, WPIX], BF16)

        BR2 = XR // BATCH
        XA = 6
        weights = sb("weights", [P, 2, TAPS, BW])
        xg = (weights[:, 1].rearrange("p k c -> p (k c)")[:, 0:XR * FG]
              .rearrange("p (s c) -> p s c", s=XR))
        st6 = sb("st6", [P, XR, 6])
        mv = sb("mv", [P, BR2, BATCH, 2])
        mg = sb("mg", [P, BR2, BATCH, 2])
        spread = sb("spread", [P, BR2, BATCH])
        dev, dev2, vare, rstd, nbias = (sb(n, [P, BR2, BATCH])
                                        for n in ("dev", "dev2", "vare", "rstd", "nbias"))
        z = sb("z", [P, 2, PADC, SRC_R])
        xT, aT, gT, bm, gated = (z[:].rearrange("p s w r -> p (s w r)")[:, i * FG:(i + 1) * FG]
                                 for i in range(5))
        x_bo = sb("x_bo", [P, 2, FG])
        x1g = sb("x1g", [P, BATCH, GC, PADC])
        pad_rows = sb("pad_rows", [P, MARGIN * PADC])

        s6 = sb("s6", [P, BATCH, 6])
        mv1 = sb("mv1", [P, BR2, BATCH, 2])
        mv2 = sb("mv2", [P, GROUPS, 2])
        mg2 = sb("mg2", [P, GROUPS, 2])
        devs = sb("devs", [P, GROUPS])
        devs2 = sb("devs2", [P, GROUPS])
        vare2 = sb("vare2", [P, GROUPS])
        picked = sb("picked", [P, 2, IMGS, GPI])
        stats_c = sb("stats_c", [P, 2, IMGS])
        norm_c = sb("norm_c", [P, 2, IMGS])
        norm_band = sb("norm_band", [P, 2, IMGS, BPI])

        raw = sb("raw", [P, 2, SRC_R * PADC])
        z_hi, z_lo = (sb(n, [P, WW + 2, BR + 2], F16) for n in ("z_hi", "z_lo"))
        offs = sb("offs", [NOFF, BW])
        squares = sb("squares", [NOFF, BW])
        rest = sb("rest", [NOFF, BW])
        middle = sb("middle", [NOFF, BW], BF16)
        parts = sb("parts", [P, BW], BF16)
        coords = sb("coords", [2 * AXIS_ROWS, 2, BW], BF16)
        farthest = sb("farthest", [NOFF, BANDS])
        dist = sb("dist", [P, 2, 2, BW])
        hats = sb("hats", [P, 2, 2, BW])
        w_work = [weights[:, 0].rearrange("p k c -> p (k c)")[:, 0:TAPS * P],
                  weights[:, 0].rearrange("p k c -> p (k c)")[:, TAPS * P:TAPS * (P + NOFF)]]
        w_flat = [w_defs[:].rearrange("p k c -> p (k c)"),
                  w_offs[:].rearrange("p k c -> p (k c)")]
        w_his, w_los = ([part[:].rearrange("p k c -> p (k c)") for part in both]
                        for both in ((w_hi, woff_hi), (w_lo, woff_lo)))
        zT = sb("zT", [WPIX, 2, WINDOWS, P])
        samples_hi, samples_lo = (sb(n, [P, 2, TAPS, BW], F16)
                                  for n in ("samples_hi", "samples_lo"))
        res = x_bo
        y = sb("y", [P, 2, BW])

        select_all = sb("select_all", [P, NOFF, P], BF16)
        far_band = sb("far_band", [BANDS, 1])
        far_any = sb("far_any", [1, 1])
        flags = sb("flags", [1, BANDS], I32)
        any_flag = sb("any_flag", [1, 1], I32)
        norm_now = sb("norm_now", [P, 2])
        band_row = sb("band_row", [P, 1])
        row_shift = sb("row_shift", [P, 1])
        row_in = sb("row_in", [P, WW])
        row_z = sb("row_z", [P, WW])
        row_zT = sb("row_zT", [P, P])
        far_dist, far_hats, far_weights = dist[:, 0], hats[:, 0], weights[:, 1, 0]
        samples = weights[:, 0]

        in_f32 = sem("in_f32")
        in_off = sem("in_off")
        in_def = sem("in_def")
        const_set = sem("const_set")
        rows_spread = sem("rows_spread")
        rows_copied = sem("rows_copied")
        x_in = [sem(f"x_in{s}") for s in range(XR)]
        x1_out = [sem(f"x1_out{s}") for s in range(BATCH)]
        pad_set = sem("pad_set")
        pad_out = sem("pad_out")
        bn_done = sem("bn_done")
        mv_ready = sem("mv_ready")
        mean_summed = sem("mean_summed")
        mg_ready = sem("mg_ready")
        dev_ready = sem("dev_ready")
        dev2_ready = sem("dev2_ready")
        var_summed = sem("var_summed")
        vare_ready = sem("vare_ready")
        spread_ready = sem("spread_ready")
        rstd_ready = sem("rstd_ready")
        nb_ready = sem("nb_ready")
        x_turned = sem("x_turned")
        xT_ready = sem("xT_ready")
        xT_hi_ready = sem("xT_hi_ready")
        xT_lo_ready = sem("xT_lo_ready")
        abg = sem("abg")
        a_done = sem("a_done")
        b_done = sem("b_done")
        g_done = sem("g_done")
        aT_ready = sem("aT_ready")
        bm_ready = sem("bm_ready")
        gT_ready = sem("gT_ready")
        ab_done = sem("ab_done")
        gated_ready = sem("gated_ready")
        o_done = sem("o_done")
        xbo_ready = sem("xbo_ready")
        x1_ready = sem("x1_ready")
        bn2_done = sem("bn2_done")
        mv1_ready = sem("mv1_ready")
        mv2_ready = sem("mv2_ready")
        final = sem("final")

        raw_in = [sem(f"raw_in{s}") for s in range(2)]
        res_in = [sem(f"res_in{s}") for s in range(2)]
        z_ready = sem("z_ready")
        z_hi_ready = sem("z_hi_ready")
        z_lo_ready = sem("z_lo_ready")
        off_done = sem("off_done")
        off_biased = sem("off_biased")
        off_chain = sem("off_chain")
        parts_ready = sem("parts_ready")
        coords_in = [sem(f"coords_in{s}") for s in range(2)]
        coord_done = sem("coord_done")
        dist_ready = sem("dist_ready")
        hats_ready = sem("hats_ready")
        weights_ready = sem("weights_ready")
        z_turned = sem("z_turned")
        zT_a = sem("zT_a")
        zT_v = sem("zT_v")
        sampled = sem("sampled")
        samples_ready = sem("samples_ready")
        lows_ready = sem("lows_ready")
        squared = sem("squared")
        scaling = sem("scaling")
        conv_done = sem("conv_done")
        y_ready = sem("y_ready")
        y_out = [sem(f"y_out{s}") for s in range(2)]

        far_step = sem("far_step")
        flags_ready = sem("flags_ready")
        waits_taken = sem("waits_taken")
        band_row_set = sem("band_row_set")
        g_raw_in, g_row_in, g_res_in, g_y_out = (sem(f"g_{n}") for n in ("raw_in", "row_in",
                                                                         "res_in", "y_out"))
        g_off_done, g_row_turned, g_coord_done, g_sampled, g_conv_done = (
            sem(f"g_{n}") for n in ("off_done", "row_turned", "coord_done", "sampled", "conv_done"))
        g_step, g_z_ready, g_coords_ready, g_row_ready, g_zT_ready = (
            sem(f"g_{n}") for n in ("step", "z_ready", "coords_ready", "row_ready", "zT_ready"))
        g_weights_ready, g_added, g_y_ready = (
            sem(f"g_{n}") for n in ("weights_ready", "added", "y_ready"))

        def after_wait(eng):
            eng.sem_inc(waits_taken, 1)

        def general(eng, band, per_band, at_start=None, before_image=None, before_band=None):
            eng.wait_ge(flags_ready, 2)
            needed = eng.value_load(any_flag[:], min_val=0, max_val=1)
            with eng.If(needed != 0):
                if at_start:
                    at_start()
                with eng.Fori(0, IMGS) as img:
                    if before_image:
                        before_image()
                    with eng.Fori(0, BPI) as b:
                        n = img * BPI + b
                        if before_band:
                            before_band(img, n)
                        flag = eng.value_load(flags[0:1, bass.ds(n, 1)], min_val=0, max_val=1)
                        with eng.If(flag != 0):
                            band(img, b, n)
                        with eng.Else():
                            for semaphore, count in per_band:
                                eng.sem_inc(semaphore, count)

        x_groups = x.rearrange("b (g f) h w -> (b g) h f w", f=GC)
        x1_groups = x1_pad.rearrange("b (g f) r w -> (b g) r f w", f=GC)
        out_v = out.rearrange("b c h w -> b c (h w)")

        def batch_ahead(g, s):
            if s % BATCH != 2:
                return None
            if isinstance(g, int):
                c = g // BATCH + 1
                return (c, c % BR2) if c < GROUPS // BATCH else None
            return ((g - s) // BATCH + s // BATCH + 1, (s // BATCH + 1) % BR2)

        B_T, B_A, B_B, B_G, B_AB, B_O, B_ST, B_W = range(8)
        B_ZT, B_S = (4, 5), (6, 7)
        B_OFF, B_CONV = B_ZT

        def zT_copied(n, g):
            a = sum(1 for h in range(g + 1) if h % 2 == 0)
            v = g + 1 - a
            na = (TGROUPS + 1) // 2
            return n * na + a, n * (TGROUPS - na) + v

        def sampled_pair(b):
            return bank[B_S[b]][:, 0:TAPS * 2 * WC * BR].rearrange("p (k c) -> p k c", k=TAPS)

        ORDER = [(step[0], int(step[1:])) for step in (
            "z0 Z0 k0 k1 s0 s1 c0 c1 k2 O0 k3 c2 s2 P0 s3 c3 c4 c5 k4 s4 c6 k5 c7 c8 k6 s5 "
            "s6 T0 T1 k7 s7 s8 k8 T2 T3 s9 s10 T4 T5 R0").split()]

        def spread_count(n, u):
            return 96 * (n // 2 + 1) if isinstance(n, int) else (n - u) * 48 + 96

        def bands(eng, stages, prologue):
            prologue()

            def band(n, u):
                for kind, j in ORDER:
                    ahead = {"c": -1, "k": 1, "s": 0, "T": 1, "z": 2, "O": 2, "P": 2,
                             "R": 2, "Z": 2}[kind]
                    if isinstance(n, int) and not 0 <= n + ahead < BANDS:
                        continue
                    if kind in stages:
                        stages[kind](n + ahead, (u + ahead) % 2, j)

            over(eng, 3, 4, BANDS + 1, 2, band)

        block = ctx.enter_context(nc.Block())

        @block.sync
        def _(sp):
            def load_x(g, s):
                wait(sp, x_turned, g - XR + 1)
                wait(sp, xbo_ready, g - XR + 1)
                sp.dma_start(xg[:, s, :].rearrange("p (f w) -> p f w", f=GC),
                             x_groups[bass.ds(g, 1)].rearrange("g h f w -> (g h) f w")
                             ).then_inc(x_in[s], 16)

            for g in range(BATCH):
                load_x(g, g)
            for dst, src in ((w_abg[:, 0], Wa), (w_abg[:, 1], Wb), (w_abg[:, 2], Wg), (w_o[:], Wo),
                             (bias_a[:], ba.rearrange("(p a) -> p a", a=1)),
                             (bias_g[:], bg.rearrange("(p a) -> p a", a=1)),
                             (row_b[:], bb.rearrange("(a p) -> a p", a=1)),
                             (row_o[:], bo.rearrange("(a p) -> a p", a=1)),
                             (ident[:], ident_d), (group_mask[:], group_mask_d)):
                sp.dma_start(dst, src).then_inc(in_f32, 16)
            for g in range(BATCH, XR):
                load_x(g, g)
            for dst, src in ((w_offs[:], w_off), (bias_off[:], b_off.rearrange("(p a) -> p a", a=1)),
                             (select[:], select_d)):
                sp.dma_start(dst, src).then_inc(in_off, 16)
            for s in range(2):
                for axis in range(2):
                    at = axis * AXIS_ROWS + OWN
                    sp.dma_start(coords[at:at + 2, s, :],
                                 coords_d[0:2 + axis:1 + axis, :]).then_inc(in_off, 16)
            sp.wait_ge(const_set, 7)
            sp.dma_start(parts[CONE:KROWS, :], coords_d).then_inc(in_off, 16)
            sp.dma_start(w_defs[:], w_def).then_inc(in_def, 16)
            sp.dma_start(select_all[:], select_all_d).then_inc(in_def, 16)
            sp.wait_ge(pad_set, 1)
            for b in range(IMGS):
                for r in (0, PADR - MARGIN):
                    sp.dma_start(x1_pad[b, :, r:r + MARGIN, :].rearrange("c r w -> c (r w)"),
                                 pad_rows[:]).then_inc(pad_out, 16)

            def store_x1(g, s):
                wait(sp, x1_ready, g + 1)
                sp.dma_start(x1_groups[bass.ds(g, 1), MARGIN:MARGIN + HH]
                             .rearrange("g r f w -> (g r) f w"),
                             x1g[:, s % BATCH]).then_inc(x1_out[s % BATCH], 16)

            def group(g, s):
                if not isinstance(g, int) or g + XR < GROUPS:
                    load_x(g + XR, s)
                if not isinstance(g, int) or g > 0:
                    store_x1(g - 1, (s - 1) % XR)

            over(sp, XR, XR, GROUPS, XR, group)
            store_x1(GROUPS - 1, (GROUPS - 1) % XR)

            for s in range(BATCH):
                sp.wait_ge(x1_out[s], 16 * GROUPS // BATCH)
            sp.wait_ge(pad_out, 16 * 2 * IMGS)

            def load_raw(n, s):
                wait(sp, z_ready, n - 1)
                sp.dma_start(raw[:, s, :],
                             x1_pad[bass.ds(n // BPI, 1), :, bass.ds(n % BPI * BR, SRC_R), :]
                             .rearrange("b c r w -> (b c) (r w)")).then_inc(raw_in[s], 16)

            def load_res(n, s):
                wait(sp, y_ready, n - 1)
                sp.dma_start(res[:, s, :].rearrange("p (r w) -> p r w", r=BR),
                             x1_pad[bass.ds(n // BPI, 1), :, bass.ds(n % BPI * BR + MARGIN, BR),
                                    MARGIN:MARGIN + WW]
                             .rearrange("b c r w -> (b c) r w")).then_inc(res_in[s], 16)

            def store_y(n, s):
                wait(sp, y_ready, n + 1)
                sp.dma_start(out_v[bass.ds(n // BPI, 1), :, bass.ds(n % BPI * BW, BW)]
                             .rearrange("b c q -> (b c) q"), y[:, s, :]).then_inc(y_out[s], 16)

            def spread_parts(n, s):
                wait(sp, parts_ready, n + 1)
                for axis in range(2):
                    for p, part in enumerate((PART0, PART1, PART2)):
                        at = axis * AXIS_ROWS + p * TAPS
                        sp.dma_start(coords[at:at + TAPS, s, :],
                                     parts[part + axis:part + NOFF:2, :]).then_inc(coords_in[s], 16)

            load_raw(0, 0)
            load_raw(1, 1)
            spread_parts(0, 0)
            load_raw(2, 0)

            def band(n, s):
                known = isinstance(n, int)
                if not known or n + 3 < BANDS:
                    load_raw(n + 3, (s + 1) % 2)
                if not known or n + 1 < BANDS:
                    spread_parts(n + 1, (s + 1) % 2)
                if not known or n >= 2:
                    store_y(n - 2, s)
                if not known or n < BANDS:
                    load_res(n, s)

            over(sp, 2, 6, BANDS + 2, 2, band)
            for s in range(2):
                sp.wait_ge(y_out[s], 16 * BANDS // 2)

            def far_band_io(img, b, n):
                sp.dma_start(raw[:, 0, :], x1_pad[bass.ds(img, 1), :, bass.ds(b * BR, SRC_R), :]
                             .rearrange("b c r w -> (b c) (r w)")).then_inc(g_raw_in, 16)
                sp.dma_start(res[:, 0, :].rearrange("p (r w) -> p r w", r=BR),
                             x1_pad[bass.ds(img, 1), :, bass.ds(b * BR + MARGIN, BR),
                                    MARGIN:MARGIN + WW]
                             .rearrange("b c r w -> (b c) r w")).then_inc(g_res_in, 16)
                with sp.Fori(0, HH) as h:
                    sp.wait_ge(g_row_ready, n * HH + h + 1)
                    sp.dma_start(row_in[:], x1_pad[bass.ds(img, 1), :, bass.ds(h + MARGIN, 1),
                                                   MARGIN:MARGIN + WW]
                                 .rearrange("b c r w -> (b c) (r w)")).then_inc(g_row_in, 16)
                sp.wait_ge(g_y_ready, n + 1)
                sp.dma_start(out_v[bass.ds(img, 1), :, bass.ds(b * BW, BW)]
                             .rearrange("b c q -> (b c) q"), y[:, 0, :]).then_inc(g_y_out, 16)
                sp.wait_ge(g_y_out, 16 * n + 16)
                after_wait(sp)

            general(sp, far_band_io, ((g_raw_in, 16), (g_res_in, 16), (g_row_in, 16 * HH),
                                      (g_y_out, 16)))

        @block.tensor
        def _(pe):
            pe.wait_ge(const_set, 2)

            def spread_rows():
                pe.wait_ge(in_f32, 160)
                nc.tensor.matmul(bank[B_B][:, 0:P], ones_row[:], row_b[:], start=True, stop=True)
                nc.tensor.matmul(bank[B_B][:, P:2 * P], ones_row[:], row_o[:], start=True,
                                 stop=True).then_inc(rows_spread, 1)

            def mean_sum(c, s):
                wait(pe, mv_ready, BATCH * (c + 1))
                wait(pe, vare_ready, c)
                nc.tensor.matmul(bank[B_ST][:, 0:2 * BATCH], average[:],
                                 mv[:, s].rearrange("p g k -> p (g k)"), start=True,
                                 stop=True).then_inc(mean_summed, 1)

            def var_sum(c, s):
                wait(pe, dev2_ready, c + 1)
                nc.tensor.matmul(bank[B_ST][:, 2 * BATCH:3 * BATCH], average[:], dev2[:, s],
                                 start=True, stop=True).then_inc(var_summed, 1)

            def turn(g, s):
                wait(pe, xT_ready, g)
                if isinstance(g, int):
                    pe.wait_ge(x_in[s], 16 * (g // XR + 1))
                else:
                    pe.wait_ge(x_in[s], (g - s) * (16 // XR) + 16)
                for f in range(GC):
                    mm = nc.tensor.transpose(bank[B_T][:, f * P:(f + 1) * P],
                                             xg[:, s, f * WW:(f + 1) * WW], ident[:])
                mm.then_inc(x_turned, 1)

            def gate(g):
                wait(pe, gated_ready, g + 1)
                wait(pe, x1_ready, g)
                for f in range(GC):
                    mm = nc.tensor.matmul(bank[B_O][:, f * P:(f + 1) * P],
                                          gated[:, f * P:(f + 1) * P], w_o[:],
                                          start=True, stop=True)
                mm.then_inc(o_done, 1)

            mean_sum(0, 0)
            var_sum(0, 0)
            spread_rows()
            pe.wait_ge(abg, 2)
            for j in range(3):
                mm = nc.tensor.transpose(bank[B_W][0:1, j * P:(j + 1) * P], abg_most[:, j:j + 1],
                                         ident[:])
            mm.then_inc(abg, 1)
            turn(0, 0)
            pe.wait_ge(abg, 4)
            nc.tensor.matmul(bank[B_W][:, 0:3], ones_row[:], abg_top[:], start=True,
                             stop=True).then_inc(abg, 1)
            pe.wait_ge(abg, ABG_STEPS)

            def group(g, s):
                known = isinstance(g, int)
                pe.wait_ge(xT_hi_ready, g + 1)
                wait(pe, aT_ready, g)
                wait(pe, gT_ready, g)
                for b, j in ((B_A, 0), (B_G, 2)):
                    nc.tensor.matmul(bank[b], w_abg_hi[:, j], xT_hi[:], start=True, stop=False)
                    nc.tensor.matmul(bank[b], w_abg_lo[:, j], xT_hi[:], start=False, stop=False)
                if not known or g + 1 < GROUPS:
                    turn(g + 1, (s + 1) % XR)
                pe.wait_ge(xT_lo_ready, g + 1)
                nc.tensor.matmul(bank[B_A], w_abg_hi[:, 0], xT_lo[:], start=False,
                                 stop=True).then_inc(a_done, 1)
                wait(pe, bm_ready, g)
                if known and g == 0:
                    pe.wait_ge(rows_copied, 1)
                for f in range(GC):
                    columns = slice(f * P, (f + 1) * P)
                    for i, (part, w) in enumerate(((xT_hi, w_abg_hi), (xT_hi, w_abg_lo),
                                                   (xT_lo, w_abg_hi))):
                        mm = nc.tensor.matmul(bank[B_B][:, columns], part[:, columns], w[:, 1],
                                              start=(i == 0), stop=(i == 2))
                mm.then_inc(b_done, 1)
                nc.tensor.matmul(bank[B_G], w_abg_hi[:, 2], xT_lo[:], start=False,
                                 stop=True).then_inc(g_done, 1)
                ahead = batch_ahead(g, s)
                if ahead:
                    mean_sum(*ahead)
                if not known or g > 0:
                    gate(g - 1)
                if ahead:
                    var_sum(*ahead)
                pe.wait_ge(aT_ready, g + 1)
                pe.wait_ge(bm_ready, g + 1)
                wait(pe, gated_ready, g)
                for f in range(GC):
                    mm = nc.tensor.matmul(bank[B_AB][:, f * P:(f + 1) * P],
                                          bm[:, f * P:(f + 1) * P], aT[:, f * P:(f + 1) * P],
                                          start=True, stop=True)
                mm.then_inc(ab_done, 1)
                if known and g == 4:
                    pe.wait_ge(scaling, 4)
                    for j in (DEF, OFF):
                        mm = nc.tensor.transpose(bank[B_W][0:1, j * P:(j + 1) * P],
                                                 w_most[:, j:j + 1], ident[:])
                    mm.then_inc(scaling, 1)
                elif known and g == 6:
                    pe.wait_ge(scaling, 6)
                    nc.tensor.matmul(bank[B_W][:, 0:2], ones_row[:], w_top[:], start=True,
                                     stop=True).then_inc(scaling, 1)

            over(pe, XR, XR, GROUPS, XR, group)
            gate(GROUPS - 1)

            pe.wait_ge(mv2_ready, GROUPS)
            nc.tensor.matmul(bank[B_ST][:, 0:2 * GROUPS], average[:],
                             mv2[:].rearrange("p g k -> p (g k)"), start=True,
                             stop=True).then_inc(final, 1)
            pe.wait_ge(final, 4)
            nc.tensor.matmul(bank[B_ST][:, 2 * GROUPS:3 * GROUPS], average[:], devs2[:],
                             start=True, stop=True).then_inc(final, 1)
            def conv(n, u, k):
                if k == 0:
                    wait(pe, lows_ready, PAIRS * (n + 1))
                    wait(pe, y_ready, n)
                    a, v = zT_copied(n + 1, TGROUPS - 1)
                    if not isinstance(n, int):
                        pe.wait_ge(zT_v, v)
                    elif n + 1 < BANDS:
                        pe.wait_ge(zT_v, v)
                for w_part, part in ((w_hi, samples_hi), (w_lo, samples_hi), (w_hi, samples_lo)):
                    mm = nc.tensor.matmul(bank[B_CONV], w_part[:, k, :], part[:, u, k, :],
                                          start=(k == 0 and (w_part, part) == (w_hi, samples_hi)),
                                          stop=(k == TAPS - 1 and part is samples_lo))
                if k == TAPS - 1:
                    mm.then_inc(conv_done, 1)

            def coordinates(n, u, k):
                b = (TAPS * u + k) % 2
                if k == 0:
                    pe.wait_ge(coords_in[u], spread_count(n, u))
                wait(pe, dist_ready, TAPS * n + k - 1)
                for d in range(2):
                    at = d * AXIS_ROWS
                    mm = nc.tensor.matmul(pairs[b][0:WPIX, d, :],
                                          select[at:at + USED_ROWS, k, :],
                                          coords[at:at + USED_ROWS, u, :], start=True, stop=True,
                                          tile_position=(at, 0))
                mm.then_inc(coord_done, 1)

            def sample(n, u, p):
                b = (PAIRS * u + p) % 2
                if p == 0:
                    wait(pe, weights_ready, TAPS * (n + 1))
                    a, v = zT_copied(n, TGROUPS - 1)
                    pe.wait_ge(zT_a, a)
                    pe.wait_ge(zT_v, v)
                wait(pe, lows_ready, PAIRS * n + p - 1)
                for w in (2 * p, 2 * p + 1):
                    cols = min(WC, WW - w * WC)
                    at = (w % 2) * BR * WC
                    mm = nc.tensor.matmul(
                        sampled_pair(b)[:, :, at:at + BR * cols],
                        zT[:, u, w, :],
                        weights[0:WPIX, u, :, w * WC * BR:(w * WC + cols) * BR],
                        start=True, stop=True)
                mm.then_inc(sampled, 1)

            def turn_windows(n, u, g):
                if g == 0:
                    wait(pe, z_ready, n + 1)
                    m = n + 1 if not isinstance(n, int) or n + 1 < BANDS else n
                    pe.wait_ge(off_biased, m + 1)
                    pe.wait_ge(off_chain, OFF_CHAIN * m + 3)
                elif g == 1:
                    wait(pe, y_ready, n - 1)
                else:
                    a, v = zT_copied(n, g - 2)
                    pe.wait_ge(*((zT_a, a) if g % 2 == 0 else (zT_v, v)))
                ws = range(4 * g, min(4 * g + 4, WINDOWS))
                for w in ws:
                    mm = nc.tensor.transpose(
                        bank[B_ZT[g % 2]][0:WPIX, (w % 4) * P:(w % 4 + 1) * P],
                        z[:, u, w * WC:w * WC + SRC_C, :].rearrange("p w r -> p (w r)"),
                        ident[:])
                mm.then_inc(z_turned, 1)

            def convolve_offsets(u):
                q = 4
                for k in range(TAPS):
                    ky, kx = k // 3, k % 3
                    at = 32 * (k % q)
                    mm = nc.tensor.matmul(
                        bank[B_OFF][at:at + NOFF, :].rearrange("p (w r) -> p w r", r=BR),
                        w_offs[:, k, :],
                        z[:, u, MARGIN - 1 + kx:MARGIN - 1 + kx + WW,
                          MARGIN - 1 + ky:MARGIN - 1 + ky + BR],
                        start=(k < q), stop=(k + q >= TAPS), tile_position=(0, at))
                return mm

            def convolve_offset_parts():
                products = [(w, z_hi, k) for w in (woff_hi, woff_lo) for k in range(TAPS)]
                products += [(woff_hi, z_lo, k) for k in range(TAPS)]
                q = 4
                for i, (w, pixels, k) in enumerate(products):
                    ky, kx = k // 3, k % 3
                    at = 32 * (i % q)
                    mm = nc.tensor.matmul(
                        bank[B_OFF][at:at + NOFF, :].rearrange("p (w r) -> p w r", r=BR),
                        w[:, k, :], pixels[:, kx:kx + WW, ky:ky + BR],
                        start=(i < q), stop=(i + q >= len(products)), tile_position=(0, at))
                return mm

            def offsets(n, u, _):
                wait(pe, z_lo_ready, n + 1)
                if not isinstance(n, int) or n > 1:
                    pe.wait_ge(zT_a, zT_copied(n - 2, TGROUPS - 2)[0])
                elif n == 1:
                    pe.wait_ge(off_chain, 3)
                convolve_offset_parts().then_inc(off_done, 1)

            def prologue():
                pe.wait_ge(in_off, 16 * 8)
                pe.wait_ge(scaling, W_STEPS)
                offsets(0, 0, 0)
                offsets(1, 1, 0)
                for g in range(TGROUPS):
                    turn_windows(0, 0, g)
                for k in range(TAPS):
                    coordinates(0, 0, k)

            bands(pe, {"c": conv, "k": coordinates, "s": sample, "T": turn_windows,
                       "O": offsets}, prologue)

            pe.wait_ge(far_step, 1)
            nc.tensor.transpose(bank[B_OFF][0:BANDS, 0:NOFF], farthest[:],
                                ident[0:NOFF, 0:NOFF]).then_inc(far_step, 1)
            pe.wait_ge(far_step, 3)
            nc.tensor.transpose(bank[B_OFF][0:1, 0:BANDS], far_band[:],
                                ident[0:BANDS, 0:BANDS]).then_inc(far_step, 1)

            def far_band_products(img, b, n):
                pe.wait_ge(g_z_ready, n + 1)
                convolve_offsets(0).then_inc(g_off_done, 1)
                pe.wait_ge(g_coords_ready, n + 1)
                after_wait(pe)
                with pe.Fori(0, HH) as h:
                    row = n * HH + h
                    pe.wait_ge(g_row_ready, row + 2)
                    nc.tensor.transpose(bank[B_CONV][:, 0:P], row_z[:],
                                        ident[:]).then_inc(g_row_turned, 1)
                    for k in range(TAPS):
                        for d in range(2):
                            mm = nc.tensor.matmul(pairs[0][:, d, :],
                                                  select_all[0:KROWS, 2 * k + d, :],
                                                  parts[0:KROWS, :], start=True, stop=True)
                        mm.then_inc(g_coord_done, 1)
                        if k == 0:
                            pe.wait_ge(g_zT_ready, row + 1)
                        pe.wait_ge(g_weights_ready, row * TAPS + k + 1)
                        nc.tensor.matmul(bank[B_S[0]], row_zT[:], far_weights, start=True,
                                         stop=True).then_inc(g_sampled, 1)
                pe.wait_ge(g_added, (n + 1) * HH * TAPS)
                for k in range(TAPS):
                    mm = nc.tensor.matmul(bank[B_CONV], w_defs[:, k, :], samples[:, k, :],
                                          start=(k == 0), stop=(k == TAPS - 1))
                mm.then_inc(g_conv_done, 1)
                pe.wait_ge(g_conv_done, n + 1)
                after_wait(pe)

            general(pe, far_band_products,
                    ((g_off_done, 1), (g_row_turned, HH), (g_coord_done, HH * TAPS),
                     (g_sampled, HH * TAPS), (g_conv_done, 1)))

        @block.scalar
        def _(act):
            act.wait_ge(in_f32, 160)

            def norm_x(g, s):
                wait(act, x_turned, g + 1)
                if isinstance(g, int):
                    act.wait_ge(nb_ready, g // BATCH + 1)
                else:
                    act.wait_ge(nb_ready, (g - s) // BATCH + s // BATCH + 1)
                wait(act, xT_lo_ready, g)
                nc.scalar.activation(xT[:], bank[B_T], ACT.Identity,
                                     bias=nbias[:, s // BATCH, s % BATCH:s % BATCH + 1],
                                     scale=rstd[:, s // BATCH, s % BATCH:s % BATCH + 1]
                                     ).then_inc(xT_ready, 1)

            def high_x(g):
                wait(act, xT_ready, g + 1)
                wait(act, g_done, g)
                nc.scalar.copy(xT_hi[:], xT[:]).then_inc(xT_hi_ready, 1)

            norm_x(0, 0)
            high_x(0)

            def group(g, s):
                ahead = not isinstance(g, int) or g + 1 < GROUPS
                if ahead:
                    norm_x(g + 1, (s + 1) % XR)
                act.wait_ge(a_done, g + 1)
                wait(act, ab_done, g)
                nc.scalar.activation(aT[:], bank[B_A], ACT.Identity, bias=bias_a[:],
                                     scale=abg_unscale[:, 0:1]).then_inc(aT_ready, 1)
                if ahead:
                    high_x(g + 1)
                act.wait_ge(g_done, g + 1)
                wait(act, gated_ready, g)
                nc.scalar.activation(gT[:], bank[B_G], ACT.Sigmoid, bias=bias_g[:],
                                     scale=abg_unscale[:, 2:3]).then_inc(gT_ready, 1)

            over(act, XR, XR, GROUPS, XR, group)

            def make_z(n, u, _):
                if isinstance(n, int):
                    act.wait_ge(raw_in[u], 16 * (n // 2 + 1))
                else:
                    act.wait_ge(raw_in[u], (n - u) * 8 + 16)
                wait(act, z_turned, TGROUPS * (n - 1))
                wait(act, off_done, n - 1)
                nc.scalar.activation(
                    z[:, u], raw[:, u, :].rearrange("p (r w) -> p w r", r=SRC_R), ACT.Relu,
                    bias=norm_band[:, 1].rearrange("p b n -> p (b n)")[:, bass.ds(n, 1)],
                    scale=norm_band[:, 0].rearrange("p b n -> p (b n)")[:, bass.ds(n, 1)]
                ).then_inc(z_ready, 1)
                act.wait_ge(z_ready, n + 1)
                wait(act, off_done, n)
                nc.scalar.activation(z_hi[:], z[:, u, MARGIN - 1:MARGIN + 1 + WW,
                                                MARGIN - 1:MARGIN + 1 + BR],
                                     ACT.Copy, scale=PIXEL_SCALE).then_inc(z_hi_ready, 1)

            def bias_offsets(n, u, _):
                act.wait_ge(off_done, n + 1)
                wait(act, off_chain, OFF_CHAIN * n)
                nc.scalar.activation(offs[:], bank[B_OFF][0:NOFF, :], ACT.Identity,
                                     bias=bias_off[:], scale=unscale[0:NOFF, OFF:OFF + 1]
                                     ).then_inc(off_biased, 1)

            def distances(n, u, k):
                b = (TAPS * u + k) % 2
                t = TAPS * n + k
                act.wait_ge(coord_done, t + 1)
                wait(act, hats_ready, t - 1)
                nc.scalar.activation(dist[0:WPIX, b], pairs[b][0:WPIX], ACT.Abs).then_inc(dist_ready, 1)

            def copy_samples(n, u, p):
                b = (PAIRS * u + p) % 2
                wait(act, sampled, PAIRS * n + p + 1)
                if p == 0:
                    wait(act, conv_done, n - 1)
                c0, c1 = 2 * p * WC * BR, min(2 * (p + 1) * WC * BR, BW)
                nc.scalar.activation(samples_hi[:, u, :, c0:c1], sampled_pair(b)[:, :, 0:c1 - c0],
                                     ACT.Copy, scale=PIXEL_SCALE).then_inc(samples_ready, 1)

            def copy_windows(n, u, g):
                if g % 2:
                    return
                wait(act, z_turned, TGROUPS * n + g + 1)
                if g == 0:
                    wait(act, sampled, PAIRS * (n - 1))
                c = min(4, WINDOWS - 4 * g)
                nc.scalar.copy(zT[:, u, 4 * g:4 * g + c, :].rearrange("p w c -> p (w c)"),
                               bank[B_ZT[0]][0:WPIX, 0:c * P]).then_inc(zT_a, 1)

            def prologue():
                act.wait_ge(in_off, 16 * 8)
                act.wait_ge(scaling, W_STEPS)
                act.wait_ge(final, FINAL_STEPS)
                make_z(0, 0, 0)
                make_z(1, 1, 0)
                bias_offsets(0, 0, 0)
                bias_offsets(1, 1, 0)
                for g in range(TGROUPS):
                    copy_windows(0, 0, g)
                for k in range(TAPS):
                    distances(0, 0, k)

            bands(act, {"k": distances, "s": copy_samples, "T": copy_windows, "z": make_z,
                        "O": bias_offsets}, prologue)

        @block.vector
        def _(dve):
            nc.vector.memset(average[:], 1.0 / P).then_inc(const_set, 1)
            nc.vector.memset(ones_row[:], 1.0).then_inc(const_set, 1)
            nc.vector.memset(minus_half[:], -0.5).then_inc(const_set, 1)

            def row_stats(g, s):
                if isinstance(g, int):
                    dve.wait_ge(x_in[s], 16 * (g // XR + 1))
                else:
                    dve.wait_ge(x_in[s], (g - s) * (16 // XR) + 16)
                nc.vector.bn_stats(st6[:, s, :], xg[:, s, :]).then_inc(bn_done, 1)

            def row_means(g, s):
                nc.vector.bn_aggr(mv[:, s // BATCH, s % BATCH, :], st6[:, s, :]).then_inc(mv_ready, 1)

            def deviations(c, s):
                dve.wait_ge(mean_summed, c + 1)
                nc.vector.tensor_copy(mg[:, s].rearrange("p g k -> p (g k)"),
                                      bank[B_ST][:, 0:2 * BATCH]).then_inc(mg_ready, 1)
                dve.wait_ge(mg_ready, c + 1)
                nc.vector.tensor_tensor(dev[:, s], mv[:, s, :, 0], mg[:, s, :, 0],
                                        ALU.subtract).then_inc(dev_ready, 1)
                dve.wait_ge(dev_ready, c + 1)
                nc.vector.tensor_tensor(dev2[:, s], dev[:, s], dev[:, s],
                                        ALU.mult).then_inc(dev2_ready, 1)

            def variance(c, s):
                dve.wait_ge(var_summed, c + 1)
                nc.vector.scalar_tensor_tensor(
                    out=spread[:, s], in0=bank[B_ST][:, 2 * BATCH:3 * BATCH], scalar=EPS,
                    in1=mg[:, s, :, 1], op0=ALU.add, op1=ALU.add).then_inc(spread_ready, 1)
                dve.wait_ge(spread_ready, c + 1)
                nc.vector.tensor_scalar(vare[:, s], spread[:, s], PIXEL_SCALE ** -2, None,
                                        ALU.mult).then_inc(vare_ready, 1)

            def norm_bias(c, s):
                dve.wait_ge(rstd_ready, c + 1)
                nc.vector.scalar_tensor_tensor(
                    out=nbias[:, s], in0=mg[:, s, :, 0], scalar=-1.0,
                    in1=rstd[:, s], op0=ALU.mult, op1=ALU.mult).then_inc(nb_ready, 1)

            def add_x(g, s):
                dve.wait_ge(o_done, g + 1)
                wait(dve, xbo_ready, g + 1)
                r = s % BATCH
                if isinstance(g, int):
                    wait(dve, x1_out[r], 16 * (g // BATCH))
                else:
                    dve.wait_ge(x1_out[r], (g - r) * (16 // BATCH))
                h = x1g[:, r, :, MARGIN:MARGIN + WW]
                nc.vector.tensor_tensor(
                    h, bank[B_O].rearrange("p (f w) -> p f w", f=GC),
                    x_bo[:, s % 2, :].rearrange("p (f w) -> p f w", f=GC),
                    ALU.add).then_inc(x1_ready, 1)
                dve.wait_ge(x1_ready, g + 1)
                nc.vector.bn_stats(s6[:, r, :], h).then_inc(bn2_done, 1)

            def x1_means(g, s):
                nc.vector.bn_aggr(mv1[:, s // BATCH, s % BATCH, :],
                                  s6[:, s % BATCH, :]).then_inc(mv1_ready, 1)

            def keep_x1_means(g, s):
                dve.wait_ge(mv1_ready, g + 1)
                nc.vector.tensor_copy(
                    mv2[:, bass.ds(g - (BATCH - 1), BATCH), :].rearrange("p g k -> p (g k)"),
                    mv1[:, s // BATCH].rearrange("p g k -> p (g k)")).then_inc(mv2_ready, BATCH)

            def scale_abg():
                dve.wait_ge(in_f32, 160)
                nc.vector.scalar_tensor_tensor(out=w_abg_work[:], in0=w_abg[:], scalar=-1.0,
                                               in1=w_abg[:], op0=ALU.mult,
                                               op1=ALU.max).then_inc(abg, 1)
                dve.wait_ge(abg, 1)
                nc.vector.tensor_reduce(abg_most[:], w_abg_work[:], AX.X,
                                        ALU.max).then_inc(abg, 1)
                dve.wait_ge(abg, 3)
                nc.vector.tensor_reduce(
                    abg_top[:], bank[B_W][0:1, 0:3 * P].rearrange("p (j c) -> p j c", j=3),
                    AX.X, ALU.max).then_inc(abg, 1)
                dve.wait_ge(abg, 5)
                nc.vector.tensor_scalar(abg_top_all[:], bank[B_W][:, 0:3], TINY, None,
                                        ALU.max).then_inc(abg, 1)
                dve.wait_ge(abg, 7)
                nc.vector.tensor_scalar(abg_unscale[:], abg_top_all[:],
                                        1 / (PIXEL_SCALE * WEIGHT_TOP), None, ALU.mult)
                for j in range(3):
                    ins = nc.vector.tensor_scalar(w_abg_work[:, j], w_abg[:, j],
                                                  abg_scale[:, j:j + 1], WEIGHT_TOP, ALU.mult,
                                                  ALU.mult)
                ins.then_inc(abg, 2)
                dve.wait_ge(abg, 9)
                nc.vector.tensor_copy(w_abg_hi[:], w_abg_work[:]).then_inc(abg, 1)
                dve.wait_ge(abg, 10)
                nc.vector.tensor_tensor(w_abg_lo[:], w_abg_work[:], w_abg_hi[:],
                                        ALU.subtract).then_inc(abg, 1)

            def scale_weights(g):
                if g == 2:
                    dve.wait_ge(in_def, 32)
                    dve.wait_ge(in_off, 16 * 8)
                    for j in (DEF, OFF):
                        nc.vector.scalar_tensor_tensor(
                            out=w_work[j], in0=w_flat[j], scalar=-1.0, in1=w_flat[j],
                            op0=ALU.mult, op1=ALU.max).then_inc(scaling, 1)
                elif g == 3:
                    dve.wait_ge(scaling, 2)
                    for j in (DEF, OFF):
                        nc.vector.tensor_reduce(w_most[:, j:j + 1], w_work[j], AX.X,
                                                ALU.max).then_inc(scaling, 1)
                elif g == 5:
                    dve.wait_ge(scaling, 5)
                    nc.vector.tensor_reduce(
                        w_top[:], bank[B_W][0:1, 0:2 * P].rearrange("p (j c) -> p j c", j=2),
                        AX.X, ALU.max).then_inc(scaling, 1)
                elif g == 7:
                    dve.wait_ge(scaling, 7)
                    nc.vector.tensor_scalar(w_top_all[:], bank[B_W][:, 0:2], TINY, None,
                                            ALU.max).then_inc(scaling, 1)

            for g in range(XA):
                row_stats(g, g)
                dve.wait_ge(bn_done, g + 1)
                row_means(g, g)
                if g == BATCH - 1:
                    deviations(0, 0)
                    variance(0, 0)
                    norm_bias(0, 0)
                    nc.vector.memset(x1g[:], BELOW_ALL).then_inc(const_set, 1)
                    nc.vector.memset(minus_one[:], -1.0).then_inc(const_set, 1)
                    nc.vector.memset(parts[0:64, :], 0.0).then_inc(const_set, 1)
                    nc.vector.memset(parts[64:128, :], 0.0).then_inc(const_set, 1)
                    nc.vector.memset(pad_rows[:], BELOW_ALL).then_inc(pad_set, 1)
                    dve.wait_ge(rows_spread, 1)
                    nc.vector.tensor_copy(all_b[:], bank[B_B][:, 0:P])
                    nc.vector.tensor_copy(all_o[:], bank[B_B][:, P:2 * P]
                                          ).then_inc(rows_copied, 1)
                    dve.wait_ge(rows_copied, 1)
                    dve.wait_ge(const_set, 7)
                    scale_abg()

            def group(g, s):
                known = isinstance(g, int)
                ahead = not known or g + XA < GROUPS
                t = (s + XA) % XR
                behind = not known or g > 0
                batch = batch_ahead(g, s)
                if batch:
                    deviations(*batch)
                dve.wait_ge(b_done, g + 1)
                wait(dve, ab_done, g)
                nc.vector.scalar_tensor_tensor(
                    out=bm[:].rearrange("p (f l) -> p f l", f=GC),
                    in0=bank[B_B].rearrange("p (f l) -> p f l", f=GC),
                    scalar=abg_unscale[:, 1:2],
                    in1=all_b[:].rearrange("p (f l) -> p f l", f=1).broadcast_to([P, GC, P]),
                    op0=ALU.mult, op1=ALU.add).then_inc(bm_ready, 1)
                if ahead:
                    row_stats(g + XA, t)
                if batch:
                    variance(*batch)
                if behind:
                    if ahead:
                        dve.wait_ge(bn_done, g + XA + 1)
                    add_x(g - 1, (s - 1) % XR)
                if ahead:
                    if not behind:
                        dve.wait_ge(bn_done, g + XA + 1)
                    row_means(g + XA, t)
                if batch:
                    norm_bias(*batch)
                dve.wait_ge(ab_done, g + 1)
                dve.wait_ge(gT_ready, g + 1)
                wait(dve, o_done, g)
                if behind:
                    dve.wait_ge(bn2_done, g)
                nc.vector.tensor_tensor(gated[:], bank[B_AB], gT[:],
                                        ALU.mult).then_inc(gated_ready, 1)
                if behind:
                    x1_means(g - 1, (s - 1) % XR)
                    if s % BATCH == 0:
                        keep_x1_means(g - 1, (s - 1) % XR)
                if known:
                    scale_weights(g)

            over(dve, XR, XR, GROUPS, XR, group)
            last = (GROUPS - 1, (GROUPS - 1) % XR)
            add_x(*last)
            dve.wait_ge(bn2_done, GROUPS)
            x1_means(*last)
            keep_x1_means(*last)

            dve.wait_ge(final, 1)
            nc.vector.tensor_copy(mg2[:].rearrange("p g k -> p (g k)"),
                                  bank[B_ST][:, 0:2 * GROUPS]).then_inc(final, 1)
            dve.wait_ge(final, 2)
            nc.vector.tensor_tensor(devs[:], mv2[:, :, 0], mg2[:, :, 0],
                                    ALU.subtract).then_inc(final, 1)
            dve.wait_ge(final, 3)
            nc.vector.tensor_tensor(devs2[:], devs[:], devs[:], ALU.mult).then_inc(final, 1)
            dve.wait_ge(final, 5)
            nc.vector.scalar_tensor_tensor(
                out=vare2[:], in0=bank[B_ST][:, 2 * GROUPS:3 * GROUPS], scalar=EPS,
                in1=mg2[:, :, 1], op0=ALU.add, op1=ALU.add).then_inc(final, 1)
            dve.wait_ge(final, 6)
            for j, per_group in enumerate((vare2[:], mg2[:, :, 0])):
                nc.vector.tensor_tensor(
                    picked[:, j], per_group.rearrange("p (b g) -> p b g", b=IMGS),
                    group_mask[:].rearrange("p (b g) -> p b g", b=1)
                    .broadcast_to([P, IMGS, GPI]), ALU.mult).then_inc(final, 1)
            dve.wait_ge(final, 8)
            for j in range(2):
                nc.vector.tensor_reduce(stats_c[:, j, :], picked[:, j], AX.X,
                                        ALU.add).then_inc(final, 1)
            dve.wait_ge(final, 11)
            nc.vector.scalar_tensor_tensor(
                out=norm_c[:, 1, :], in0=stats_c[:, 1, :], scalar=-1.0, in1=norm_c[:, 0, :],
                op0=ALU.mult, op1=ALU.mult).then_inc(final, 1)
            dve.wait_ge(final, 12)
            for j in range(2):
                nc.vector.tensor_copy(
                    norm_band[:, j],
                    norm_c[:, j, :].rearrange("p (b n) -> p b n", n=1)
                    .broadcast_to([P, IMGS, BPI])).then_inc(final, 1)

            def make_hats(n, u, k):
                b = (TAPS * u + k) % 2
                t = TAPS * n + k
                dve.wait_ge(dist_ready, t + 1)
                wait(dve, weights_ready, t - 1)
                nc.vector.tensor_scalar(hats[0:WPIX, b], dist[0:WPIX, b], -1.0, 0.0, ALU.add,
                                        ALU.min).then_inc(hats_ready, 1)

            def copy_samples_lo(n, u, p):
                b = (PAIRS * u + p) % 2
                wait(dve, samples_ready, PAIRS * n + p + 1)
                if p == 0:
                    wait(dve, conv_done, n - 1)
                c0, c1 = 2 * p * WC * BR, min(2 * (p + 1) * WC * BR, BW)
                nc.vector.scalar_tensor_tensor(
                    out=samples_lo[:, u, :, c0:c1], in0=sampled_pair(b)[:, :, 0:c1 - c0],
                    scalar=PIXEL_SCALE, in1=samples_hi[:, u, :, c0:c1],
                    op0=ALU.mult, op1=ALU.subtract).then_inc(lows_ready, 1)

            def split_z(n, u, _):
                dve.wait_ge(z_hi_ready, n + 1)
                nc.vector.scalar_tensor_tensor(
                    out=z_lo[:], in0=z[:, u, MARGIN - 1:MARGIN + 1 + WW,
                                       MARGIN - 1:MARGIN + 1 + BR],
                    scalar=PIXEL_SCALE, in1=z_hi[:], op0=ALU.mult,
                    op1=ALU.subtract).then_inc(z_lo_ready, 1)

            def sum_offsets(n, u, _):
                for j in range(3):
                    dve.wait_ge(*((off_chain, OFF_CHAIN * n + j) if j else (off_biased, n + 1)))
                    nc.vector.scalar_tensor_tensor(
                        out=offs[:], in0=bank[B_OFF][32 * (j + 1):32 * (j + 1) + NOFF, :],
                        scalar=unscale[0:NOFF, OFF:OFF + 1], in1=offs[:], op0=ALU.mult,
                        op1=ALU.add).then_inc(off_chain, 1)

            def split_offsets(n, u, _):
                c = OFF_CHAIN * n

                def done(ins, j):
                    ins.then_inc(off_chain, 1)
                    dve.wait_ge(off_chain, c + j)

                dve.wait_ge(off_chain, c + 3)
                if not isinstance(n, int) or n > 0:
                    dve.wait_ge(coords_in[1 - u], spread_count(n - 1, 1 - u))
                done(nc.vector.tensor_copy(parts[PART0:PART0 + NOFF, :], offs[:]), 4)
                done(nc.vector.tensor_tensor(rest[:], offs[:], parts[PART0:PART0 + NOFF, :],
                                             ALU.subtract), 5)
                done(nc.vector.tensor_copy(middle[:], rest[:]), 6)
                done(nc.vector.tensor_tensor(parts[PART2:PART2 + NOFF, :], rest[:], middle[:],
                                             ALU.subtract), 7)
                nc.vector.tensor_copy(parts[PART1:PART1 + NOFF, :],
                                      middle[:]).then_inc(parts_ready, 1)

            def reach(n, u, _):
                dve.wait_ge(squared, n + 1)
                nc.vector.tensor_reduce(farthest[:, bass.ds(n, 1)], squares[:], AX.X,
                                        ALU.max).then_inc(off_chain, 1)

            def copy_windows(n, u, g):
                if g % 2 == 0:
                    return
                dve.wait_ge(z_turned, TGROUPS * n + g + 1)
                if g == 1:
                    wait(dve, sampled, PAIRS * (n - 1))
                c = min(4, WINDOWS - 4 * g)
                nc.vector.tensor_copy(zT[:, u, 4 * g:4 * g + c, :].rearrange("p w c -> p (w c)"),
                                      bank[B_ZT[1]][0:WPIX, 0:c * P]).then_inc(zT_v, 1)

            def add_x1(n, u, k):
                if k < TAPS - 1:
                    return
                dve.wait_ge(conv_done, n + 1)
                if isinstance(n, int):
                    dve.wait_ge(res_in[u], 16 * (n // 2 + 1))
                    wait(dve, y_out[u], 16 * (n // 2))
                else:
                    dve.wait_ge(res_in[u], (n - u) * 8 + 16)
                    dve.wait_ge(y_out[u], (n - u) * 8)
                nc.vector.scalar_tensor_tensor(
                    out=y[:, u, :].rearrange("p (r w) -> p r w", r=BR),
                    in0=bank[B_CONV].rearrange("p (w r) -> p r w", r=BR), scalar=unscale[:, DEF:DEF + 1],
                    in1=res[:, u, :].rearrange("p (r w) -> p r w", r=BR),
                    op0=ALU.mult, op1=ALU.add).then_inc(y_ready, 1)

            def prologue():
                dve.wait_ge(scaling, W_STEPS)
                split_z(0, 0, 0)
                split_z(1, 1, 0)
                sum_offsets(0, 0, 0)
                split_offsets(0, 0, 0)
                reach(0, 0, 0)
                sum_offsets(1, 1, 0)
                for g in range(TGROUPS):
                    copy_windows(0, 0, g)
                for k in range(TAPS):
                    if k == 3:
                        split_offsets(1, 1, 0)
                        reach(1, 1, 0)
                    make_hats(0, 0, k)

            bands(dve, {"c": add_x1, "k": make_hats, "s": copy_samples_lo, "T": copy_windows, "O": sum_offsets,
                        "P": split_offsets, "R": reach, "Z": split_z}, prologue)

            dve.wait_ge(off_chain, OFF_CHAIN * BANDS)
            after_wait(dve)
            dve.sem_inc(far_step, 1)
            dve.wait_ge(far_step, 2)
            nc.vector.tensor_reduce(far_band[:], bank[B_OFF][0:BANDS, 0:NOFF], AX.X,
                                    ALU.max).then_inc(far_step, 1)
            dve.wait_ge(far_step, 4)
            nc.vector.tensor_reduce(far_any[:], bank[B_OFF][0:1, 0:BANDS], AX.X,
                                    ALU.max).then_inc(far_step, 1)
            nc.vector.tensor_scalar(flags[:], bank[B_OFF][0:1, 0:BANDS], float(REACH * REACH),
                                    None, ALU.is_gt).then_inc(flags_ready, 1)
            dve.wait_ge(far_step, 5)
            nc.vector.tensor_scalar(any_flag[:], far_any[:], float(REACH * REACH), None,
                                    ALU.is_gt).then_inc(flags_ready, 1)

            def free_row():
                dve.sem_inc(g_row_ready, 1)

            def first_row():
                nc.vector.memset(band_row[:], -1.0 - BR).then_inc(band_row_set, 1)

            def next_row(img, n):
                dve.wait_ge(band_row_set, img + n + 1)
                nc.vector.tensor_scalar(band_row[:], band_row[:], float(BR), None,
                                        ALU.add).then_inc(band_row_set, 1)
                dve.wait_ge(band_row_set, img + n + 2)
                after_wait(dve)

            def far_band_weights(img, b, n):
                steps = n * (BAND_STEPS + HH * ROW_STEPS)

                def step(ins, j, base=None):
                    ins.then_inc(g_step, 1)
                    dve.wait_ge(g_step, (steps if base is None else base) + j)

                dve.wait_ge(g_raw_in, 16 * n + 16)
                step(nc.vector.tensor_copy(
                    norm_now[:], norm_band[:].rearrange("p j b n -> p j (b n)")
                    [:, :, bass.ds(n, 1)].rearrange("p j n -> p (j n)")), 1)
                step(nc.vector.tensor_scalar(raw[:, 0, :], raw[:, 0, :], norm_now[:, 0:1],
                                             norm_now[:, 1:2], ALU.mult, ALU.add), 2)
                nc.vector.tensor_scalar(
                    z[:, 0], raw[:, 0, :].rearrange("p (r w) -> p w r", r=SRC_R), 0.0, None,
                    ALU.max).then_inc(g_z_ready, 1)
                dve.wait_ge(g_off_done, n + 1)
                step(nc.vector.tensor_scalar(offs[:], bank[B_OFF][0:NOFF, :], bias_off[:], None,
                                             ALU.add), 3)
                for j in (1, 2, 3):
                    step(nc.vector.tensor_tensor(
                        offs[:], bank[B_OFF][32 * j:32 * j + NOFF, :], offs[:], ALU.add), 3 + j)
                step(nc.vector.tensor_copy(parts[PART0:PART0 + NOFF, :], offs[:]), 7)
                step(nc.vector.tensor_tensor(rest[:], offs[:], parts[PART0:PART0 + NOFF, :],
                                             ALU.subtract), 8)
                step(nc.vector.tensor_copy(middle[:], rest[:]), 9)
                step(nc.vector.tensor_tensor(parts[PART2:PART2 + NOFF, :], rest[:], middle[:],
                                             ALU.subtract), 10)
                nc.vector.tensor_copy(parts[PART1:PART1 + NOFF, :],
                                      middle[:]).then_inc(g_coords_ready, 1)
                step(nc.vector.memset(samples[:], 0.0), 11)
                step(nc.vector.tensor_copy(row_shift[:], band_row[:]), 12)
                after_wait(dve)

                with dve.Fori(0, HH) as h:
                    row = n * HH + h
                    at = (n * (BAND_STEPS + HH * ROW_STEPS) + BAND_STEPS) + h * ROW_STEPS
                    dve.wait_ge(g_row_in, row * 16 + 16)
                    step(nc.vector.tensor_scalar(row_z[:], row_in[:], norm_now[:, 0:1],
                                                 norm_now[:, 1:2], ALU.mult, ALU.add), 1, at)
                    nc.vector.tensor_scalar(row_z[:], row_z[:], 0.0, None,
                                            ALU.max).then_inc(g_row_ready, 1)
                    dve.wait_ge(g_row_turned, row + 1)
                    nc.vector.tensor_copy(row_zT[:], bank[B_CONV][:, 0:P]).then_inc(g_zT_ready, 1)
                    for k in range(TAPS):
                        j = 1 + 4 * k
                        dve.wait_ge(g_coord_done, row * TAPS + k + 1)
                        step(nc.vector.tensor_scalar(far_dist[:, 0, :], pairs[0][:, 0, :],
                                                     row_shift[:], None, ALU.add), j + 1, at)
                        step(nc.vector.tensor_copy(far_dist[:, 1, :], pairs[0][:, 1, :]),
                             j + 2, at)
                        step(nc.vector.scalar_tensor_tensor(
                            out=far_hats, in0=far_dist, scalar=-1.0, in1=far_dist,
                            op0=ALU.mult, op1=ALU.max), j + 3, at)
                        step(nc.vector.tensor_scalar(far_hats, far_hats, -1.0, 0.0,
                                                     ALU.add, ALU.min), j + 4, at)
                        nc.vector.tensor_tensor(far_weights, far_hats[:, 0, :],
                                                far_hats[:, 1, :],
                                                ALU.mult).then_inc(g_weights_ready, 1)
                        dve.wait_ge(g_sampled, row * TAPS + k + 1)
                        nc.vector.tensor_tensor(samples[:, k, :], bank[B_S[0]],
                                                samples[:, k, :], ALU.add).then_inc(g_added, 1)
                    step(nc.vector.tensor_scalar(row_shift[:], row_shift[:], -1.0, None,
                                                 ALU.add), ROW_STEPS, at)

                dve.wait_ge(g_conv_done, n + 1)
                dve.wait_ge(g_res_in, 16 * n + 16)
                nc.vector.tensor_tensor(
                    y[:, 0, :].rearrange("p (r w) -> p r w", r=BR),
                    res[:, 0, :].rearrange("p (r w) -> p r w", r=BR),
                    bank[B_CONV].rearrange("p (w r) -> p r w", r=BR),
                    ALU.add).then_inc(g_y_ready, 1)
                dve.wait_ge(g_y_out, 16 * n + 16)
                after_wait(dve)

            general(dve, far_band_weights,
                    ((g_z_ready, 1), (g_coords_ready, 1), (g_row_ready, HH), (g_zT_ready, HH),
                     (g_weights_ready, HH * TAPS), (g_added, HH * TAPS), (g_y_ready, 1),
                     (g_step, BAND_STEPS + HH * ROW_STEPS)),
                    free_row, first_row, next_row)

        @block.gpsimd
        def _(pool):
            pool.wait_ge(const_set, 3)

            def inverse_root(c, s):
                pool.wait_ge(vare_ready, c + 1)
                nc.gpsimd.tensor_tensor(rstd[:, s], vare[:, s], minus_half[:, 0:BATCH],
                                        ALU.pow).then_inc(rstd_ready, 1)

            inverse_root(0, 0)
            pool.wait_ge(rows_copied, 1)
            pool.wait_ge(const_set, 7)
            pool.wait_ge(abg, 6)
            nc.gpsimd.tensor_tensor(abg_scale[:], abg_top_all[:], minus_one[:],
                                    ALU.pow).then_inc(abg, 1)

            def low_x(g):
                wait(pool, xT_hi_ready, g + 1)
                nc.gpsimd.tensor_tensor(xT_lo[:], xT[:], xT_hi[:],
                                        ALU.subtract).then_inc(xT_lo_ready, 1)

            low_x(0)

            def group(g, s):
                if not isinstance(g, int) or g + 1 < GROUPS:
                    low_x(g + 1)
                if isinstance(g, int):
                    pool.wait_ge(x_in[s], 16 * (g // XR + 1))
                else:
                    pool.wait_ge(x_in[s], (g - s) * (16 // XR) + 16)
                wait(pool, x1_ready, g - 1)
                nc.gpsimd.tensor_tensor(
                    x_bo[:, s % 2, :].rearrange("p (f w) -> p f w", f=GC),
                    xg[:, s, :].rearrange("p (f w) -> p f w", f=GC),
                    all_o[:].rearrange("p (f l) -> p f l", f=1).broadcast_to([P, GC, P]),
                    ALU.add).then_inc(xbo_ready, 1)
                if batch_ahead(g, s):
                    inverse_root(*batch_ahead(g, s))
                step = g - (GROUPS - XR) if isinstance(g, int) else None
                if step == 0:
                    pool.wait_ge(scaling, 8)
                    nc.gpsimd.tensor_tensor(w_scale[:], w_top_all[:], minus_one[:, 0:2],
                                            ALU.pow).then_inc(scaling, 1)
                elif step == 1:
                    pool.wait_ge(scaling, 9)
                    for j in (DEF, OFF):
                        nc.gpsimd.tensor_scalar(
                            w_work[j], w_flat[j], w_scale[:, j:j + 1], WEIGHT_TOP,
                            ALU.mult, ALU.mult).then_inc(scaling, 1)
                elif step == 2:
                    pool.wait_ge(scaling, 11)
                    for j in (DEF, OFF):
                        nc.gpsimd.tensor_copy(w_his[j], w_work[j]).then_inc(scaling, 1)
                elif step == 3:
                    pool.wait_ge(scaling, 13)
                    for j in (DEF, OFF):
                        nc.gpsimd.tensor_tensor(w_los[j], w_work[j], w_his[j],
                                                ALU.subtract).then_inc(scaling, 1)
                    nc.gpsimd.tensor_scalar(
                        unscale[:], w_top_all[:], 1 / (PIXEL_SCALE * WEIGHT_TOP), None,
                        ALU.mult).then_inc(scaling, 1)

            over(pool, XR, XR, GROUPS, XR, group)

            pool.wait_ge(final, 10)
            nc.gpsimd.tensor_tensor(norm_c[:, 0, :], stats_c[:, 0, :], minus_half[:, 0:IMGS],
                                    ALU.pow).then_inc(final, 1)

            def weigh(n, u, k):
                b = (TAPS * u + k) % 2
                pool.wait_ge(hats_ready, TAPS * n + k + 1)
                if k == 0:
                    wait(pool, sampled, PAIRS * (n - 1))
                nc.gpsimd.tensor_tensor(weights[0:WPIX, u, k, :], hats[0:WPIX, b, 0, :],
                                        hats[0:WPIX, b, 1, :], ALU.mult).then_inc(weights_ready, 1)

            def square_offsets(n, u, _):
                pool.wait_ge(off_chain, OFF_CHAIN * n + 3)
                nc.gpsimd.tensor_tensor(squares[:], offs[:], offs[:],
                                        ALU.mult).then_inc(squared, 1)

            def prologue():
                square_offsets(0, 0, 0)
                for k in range(TAPS):
                    if k == 3:
                        square_offsets(1, 1, 0)
                    weigh(0, 0, k)

            bands(pool, {"k": weigh, "P": square_offsets}, prologue)


def kernel(x, L0_conv_Wa, L0_conv_ba, L0_conv_Wb, L0_conv_bb, L0_conv_Wg, L0_conv_bg, L0_conv_Wo,
           L0_conv_bo, L1_conv_w_off, L1_conv_b_off, L1_conv_w_def):
    import ml_dtypes
    import numpy as np
    import concourse.bacc as bacc
    from concourse.bass_utils import run_bass_kernel_spmd

    chan = np.arange(CH)
    group_mask = (chan[:, None] // GC == np.arange(GPI)[None]).astype(np.float32)
    select = np.zeros((2 * AXIS_ROWS, TAPS, WPIX), np.float32)
    select_all = np.zeros((P, NOFF, P), np.float32)
    q = np.arange(WPIX)
    for k in range(TAPS):
        for d in range(2):
            j = 2 * k + d
            for p, part in enumerate((PART0, PART1, PART2)):
                select[d * AXIS_ROWS + p * TAPS + k, k] = 1
                select_all[part + j, j] = 1
            shift = (k // 3, k % 3)[d]
            own = (q % SRC_R, q // SRC_R)[d]
            select[d * AXIS_ROWS + OWN, k] = REACH + shift - own
            select[d * AXIS_ROWS + OWN + 1, k] = 1
            select_all[CONE, j] = (0, -1)[d] + shift - (0, 1)[d] * np.arange(P)
            select_all[CONE + (1, 3)[d], j] = 1
    w, r = np.divmod(np.arange(BW), BR)
    coords = np.stack([np.ones(BW), r, w % WC, w]).astype(ml_dtypes.bfloat16)

    arrays = {
        "x": x, "Wa": L0_conv_Wa, "ba": L0_conv_ba, "Wb": L0_conv_Wb, "bb": L0_conv_bb,
        "Wg": L0_conv_Wg, "bg": L0_conv_bg, "Wo": L0_conv_Wo, "bo": L0_conv_bo,
        "w_off": np.asarray(L1_conv_w_off).reshape(NOFF, CH, TAPS).transpose(1, 2, 0),
        "b_off": L1_conv_b_off,
        "w_def": np.asarray(L1_conv_w_def).reshape(P, CH, TAPS).transpose(1, 2, 0),
        "ident": np.eye(P, dtype=np.float32), "group_mask": group_mask,
        "select": select.astype(ml_dtypes.bfloat16),
        "select_all": select_all.astype(ml_dtypes.bfloat16), "coords": coords,
    }
    arrays = {f"in_{n}": np.ascontiguousarray(a) for n, a in arrays.items()}
    nc = bacc.Bacc("TRN2", target_bir_lowering=False, num_devices=1)
    args = [nc.dram_tensor(n, a.shape, mybir.dt.from_np(a.dtype), kind="ExternalInput").ap()
            for n, a in arrays.items()]
    out = nc.dram_tensor("out", (IMGS, CH, HH, WW), F32, kind="ExternalOutput").ap()
    preact_conv_kernel(nc, *args, out)
    return run_bass_kernel_spmd(nc, [arrays], core_ids=[0]).results[0]["out"]
```
